# Optimizing a Trainium2 kernel written in Bass

```python
import numpy as np
import jax
import jax.numpy as jnp

def _softmax(x, axis=-1):
    return jax.nn.softmax(x, axis=axis)

def _gelu(x):
    return jax.nn.gelu(x, approximate=True)

def _silu(x):
    return jax.nn.silu(x)

def _sigmoid(x):
    return jax.nn.sigmoid(x)

def _layernorm(x, axis=-1, eps=1e-05):
    m = jnp.mean(x, axis=axis, keepdims=True)
    v = jnp.var(x, axis=axis, keepdims=True)
    return (x - m) / jnp.sqrt(v + eps)

def _scatter_add(tgt, idx, src, axis=0):
    return tgt.at[idx].add(src)

def _segment_sum(src, seg, n):
    return jax.ops.segment_sum(src, seg, n)
kernel_name = 'mk_adaln_ffn_d1_seqx_r8_47e52d'

def setup_inputs(seed: int=0):
    np.random.seed(seed)
    _w = jnp.asarray

    def _rec_inputs():
        import jax
        import jax.numpy as jnp
        _rk = jax.random.key(seed)
        x = -0.000125 + 0.9999 * jax.random.normal(jax.random.fold_in(_rk, 1), (8, 128, 512), jnp.float32)
        _lenS = 128 - jax.random.randint(jax.random.fold_in(_rk, 7), (8,), 0, max(1, 128 // 4) + 1, jnp.int32)
        _lenS2 = 128 - jax.random.randint(jax.random.fold_in(_rk, 8), (8,), 0, max(1, 128 // 4) + 1, jnp.int32)
        itok_B_0_7 = jax.random.randint(jax.random.fold_in(_rk, 11), (8,), 0, 8, jnp.int32)
        return (x, itok_B_0_7)
    x, itok_B_0_7 = _rec_inputs()

    def _L0_cond_setup():
        import jax, jax.numpy as jnp
        import numpy as np
        TOP_K = 2
        LANG_BIAS = 5.0
        SCALING = 32.0 / 16.0
        LANGUAGE_PAD_ID = -1
        key = jax.random.key(seed)
        ks = jax.random.split(key, 6)
        B, T, D, O, E, R = (4, 256, 512, 512, 8, 16)
        x = jax.random.normal(ks[0], (B, T, D), dtype=jnp.float32)
        language_ids = jax.random.randint(ks[1], (B,), 0, E).astype(jnp.int64)
        W = jax.random.normal(ks[2], (O, D), dtype=jnp.float32) * (1.0 / np.sqrt(D))
        Wr = jax.random.normal(ks[3], (E, D), dtype=jnp.float32) * (1.0 / np.sqrt(D))
        A = jax.random.normal(ks[4], (E, R, D), dtype=jnp.float32) * (1.0 / np.sqrt(D))
        Bm = jax.random.normal(ks[5], (O, R), dtype=jnp.float32) * 0.0
        Bm = jnp.broadcast_to(Bm, (E, O, R)) + jax.random.normal(ks[5], (E, O, R), dtype=jnp.float32) * 0.02
        return {'x': x, 'language_ids': language_ids, 'W': W, 'Wr': Wr, 'A': A, 'B': Bm}
    _L0_cond_all = _L0_cond_setup()
    _L0_cond_in = {k: v for k, v in _L0_cond_all.items() if k in ('W', 'Wr', 'A', 'B')}
    del _L0_cond_all

    def _L0_ffn_setup():
        import jax, jax.numpy as jnp
        import numpy as np
        MAX_THRESHOLD = 1.0 / 8.0
        SCALING = 32.0 / 16.0
        key = jax.random.key(seed)
        ks = jax.random.split(key, 8)
        B_, S, D, O, E, R = (4, 256, 512, 512, 8, 16)
        sd = 1.0 / np.sqrt(D)
        return {'x': jax.random.normal(ks[0], (B_, S, D), jnp.float32), 'W_base': jax.random.normal(ks[1], (O, D), jnp.float32) * sd, 'b_base': jax.random.normal(ks[2], (O,), jnp.float32) * 0.01, 'W_gate': jax.random.normal(ks[3], (E, D), jnp.float32) * sd, 'W_thr': jax.random.normal(ks[4], (1, D), jnp.float32) * sd, 'b_thr': jax.random.normal(ks[5], (1,), jnp.float32) * 0.01, 'A': jax.random.normal(ks[6], (E, R, D), jnp.float32) * sd, 'B': jax.random.normal(ks[7], (O,), jnp.float32)[None, :, None] * jnp.zeros((E, O, R), jnp.float32) + jax.random.normal(jax.random.fold_in(key, 7), (E, O, R), jnp.float32) * (1.0 / np.sqrt(R))}
    _L0_ffn_all = _L0_ffn_setup()
    _L0_ffn_in = {k: v for k, v in _L0_ffn_all.items() if k in ('W_base', 'b_base', 'W_gate', 'W_thr', 'b_thr', 'A', 'B')}
    del _L0_ffn_all
    return {'x': x, 'itok_B_0_7': itok_B_0_7, 'L0_cond_W': _L0_cond_in['W'], 'L0_cond_Wr': _L0_cond_in['Wr'], 'L0_cond_A': _L0_cond_in['A'], 'L0_cond_B': _L0_cond_in['B'], 'L0_ffn_W_base': _L0_ffn_in['W_base'], 'L0_ffn_b_base': _L0_ffn_in['b_base'], 'L0_ffn_W_gate': _L0_ffn_in['W_gate'], 'L0_ffn_W_thr': _L0_ffn_in['W_thr'], 'L0_ffn_b_thr': _L0_ffn_in['b_thr'], 'L0_ffn_A': _L0_ffn_in['A'], 'L0_ffn_B': _L0_ffn_in['B']}

def reference(x, itok_B_0_7, L0_cond_W, L0_cond_Wr, L0_cond_A, L0_cond_B, L0_ffn_W_base, L0_ffn_b_base, L0_ffn_W_gate, L0_ffn_W_thr, L0_ffn_b_thr, L0_ffn_A, L0_ffn_B):
    import jax
    import jax.numpy as jnp

    def _L0_cond_ref(x, language_ids, W, Wr, A, B):
        import jax, jax.numpy as jnp
        import numpy as np
        TOP_K = 2
        LANG_BIAS = 5.0
        SCALING = 32.0 / 16.0
        LANGUAGE_PAD_ID = -1
        base = jnp.einsum('btd,od->bto', x, W)
        E = Wr.shape[0]
        logits = jnp.einsum('btd,ed->bte', x.astype(jnp.float32), Wr.astype(jnp.float32))
        expert_targets = language_ids
        valid = expert_targets >= 0
        tgt = jnp.where(valid, expert_targets, 0)
        bias = jax.nn.one_hot(tgt, E, dtype=logits.dtype) * LANG_BIAS
        bias = jnp.where(valid[:, None], bias, 0.0)
        logits = logits + bias[:, None, :]
        topw, topi = jax.lax.top_k(logits, TOP_K)
        weights = jax.nn.softmax(topw, axis=-1)
        gates = jnp.sum(jax.nn.one_hot(topi, E, dtype=weights.dtype) * weights[..., None], axis=-2)
        gates = gates.astype(x.dtype)
        h = jnp.einsum('btd,erd->bter', x, A)
        lora_out = jnp.einsum('bter,bte,eor->bto', h, gates, B)
        return base + SCALING * lora_out

    def _L0_ffn_ref(x, W_base, b_base, W_gate, W_thr, b_thr, A, B):
        import jax, jax.numpy as jnp
        import numpy as np
        MAX_THRESHOLD = 1.0 / 8.0
        SCALING = 32.0 / 16.0
        base = jnp.einsum('bsd,od->bso', x, W_base) + b_base
        D = x.shape[-1]
        xf = x.reshape(-1, D)
        gate_logits = jax.nn.softmax(xf @ W_gate.T, axis=-1)
        thresholds = jax.nn.sigmoid(xf @ W_thr.T + b_thr) * MAX_THRESHOLD
        adapted = gate_logits - thresholds
        selected = (adapted >= 0).astype(x.dtype)
        weights = adapted * selected
        wsum = jnp.sum(weights, axis=-1, keepdims=True)
        wsum = jnp.where(wsum == 0, jnp.ones_like(wsum), wsum)
        weights = weights / wsum
        h = jnp.einsum('nd,erd->ner', xf, A)
        moe = jnp.einsum('ner,ne,eor->no', h, weights, B) * SCALING
        out = base + moe.reshape(base.shape)
        return out
    x = x + _L0_ffn_ref(_L0_cond_ref(x, itok_B_0_7, L0_cond_W, L0_cond_Wr, L0_cond_A, L0_cond_B), L0_ffn_W_base, L0_ffn_b_base, L0_ffn_W_gate, L0_ffn_W_thr, L0_ffn_b_thr, L0_ffn_A, L0_ffn_B)
    return x

_drawn_inputs = setup_inputs


def setup_inputs(seed=0):
    import zlib

    import numpy as np

    out = dict(_drawn_inputs(seed))
    spreads = {}
    factors = {'L0_cond_Wr': 3.542, 'L0_ffn_b_base': 8.0}
    for name, (base, spread) in spreads.items():
        noise = np.random.default_rng([zlib.crc32(name.encode()), seed]).standard_normal(out[name].shape)
        drawn = base * np.exp(spread * noise) if base else spread * noise
        out[name] = jnp.asarray(drawn.astype(out[name].dtype))
    for name, factor in factors.items():
        out[name] = (out[name] * factor).astype(out[name].dtype)
    return out
```

```python
from contextlib import ExitStack

import concourse.bass as bass
from concourse import mybir

ALU = mybir.AluOpType
ACT = mybir.ActivationFunctionType
AX = mybir.AxisListType
F32 = mybir.dt.float32
F32R = mybir.dt.float32r
I32 = mybir.dt.int32

P = 128
LANG_BIAS = 5.0
SCALING = 2.0
MAX_THRESHOLD = 0.125
MASKED = -3.0e38


def adaln_ffn_kernel(nc, x, itok, W, Wr, A1, B1, Wb, b_base, Wg, Wt, b_thr, A2, B2, out):
    NB, S, D = x.shape
    O = W.shape[0]
    E, R, _ = A1.shape
    ER = E * R
    T = NB * S // P
    K = D // P
    Q = O // P
    assert S == P and ER == P and D == O
    C_R = ER
    C_X = ER + E
    NX = ER + E + 1
    NAUX = C_X + NX + 1
    PAIR = 2

    x_tiles = x.rearrange("b s d -> (b s) d").rearrange("(t p) d -> t p d", p=P)
    out_tiles = out.rearrange("b s d -> (b s) d").rearrange("(t p) d -> t p d", p=P)
    W_rows = W.rearrange("(p q) d -> p q d", q=Q)
    B1_rows = B1.rearrange("e (p q) r -> p e (q r)", q=Q)
    B2_rows = B2.rearrange("e (p q) r -> p e (q r)", q=Q)
    Wb_rows = Wb.rearrange("(c p) o -> p c o", p=P)
    A1_rows = A1.rearrange("e r d -> (e r) d")
    A2_rows = A2.rearrange("e r d -> (e r) d")

    ctx = ExitStack()
    with ctx:
        def sb(name, shape, dt=F32):
            return ctx.enter_context(nc.sbuf_tensor(name, shape, dt))

        def sem(name):
            return ctx.enter_context(nc.semaphore(name))

        x_sb = sb("x_sb", [P, T, D])
        W_sb = sb("W_sb", [P, Q, D])
        Wb_sb = sb("Wb_sb", [P, Q, O])
        A1_sb = sb("A1_sb", [P, D])
        A2_sb = sb("A2_sb", [P, O])
        B1_sb = sb("B1_sb", [P, E, Q * R])
        B2_sb = sb("B2_sb", [P, E, Q * R])
        B1_pack = sb("B1_pack", [P, Q, ER])
        B2_pack = sb("B2_pack", [P, Q, ER])
        Wr_sb = sb("Wr_sb", [E, D])
        Wgt_sb = sb("Wgt_sb", [E + 1, O])
        b_sb = sb("b_sb", [P, D])
        bthr_sb = sb("bthr_sb", [P, 1])
        itok_sb = sb("itok_sb", [P, T], I32)

        ident = sb("ident", [P, P])
        xT_hi = sb("xT_hi", [P, K, T * P], F32R)
        xT_lo = sb("xT_lo", [P, K, T * P], F32R)
        W_hi = sb("W_hi", [P, Q, D], F32R)
        W_lo = sb("W_lo", [P, Q, D], F32R)
        WbT_hi = sb("WbT_hi", [P, Q, O], F32R)
        WbT_lo = sb("WbT_lo", [P, Q, O], F32R)
        M2auxT = sb("M2auxT", [P, Q, NX])
        aux_hi = sb("aux_hi", [P, K, NAUX], F32R)
        aux_lo = sb("aux_lo", [P, K, NAUX], F32R)
        B1_hi = sb("B1_hi", [P, Q, ER], F32R)
        B1_lo = sb("B1_lo", [P, Q, ER], F32R)
        F_hi = sb("F_hi", [P, K, O], F32R)
        F_lo = sb("F_lo", [P, K, O], F32R)
        G_aux = sb("G_aux", [P, NX])
        G_hi = sb("G_hi", [P, O], F32R)
        G_lo = sb("G_lo", [P, O], F32R)
        B2T_hi = sb("B2T_hi", [P, O], F32R)
        B2T_lo = sb("B2T_lo", [P, O], F32R)
        hgT = sb("hgT", [P, T * P])
        hgT_hi = sb("hgT_hi", [P, T * P], F32R)
        hgT_lo = sb("hgT_lo", [P, T * P], F32R)
        hwT_hi = sb("hwT_hi", [P, T * P], F32R)
        hwT_lo = sb("hwT_lo", [P, T * P], F32R)

        xaux = sb("xaux", [P, T, NAUX - 1])
        y2 = sb("y2", [P, T, NX])
        hg = sb("hg", [P, T, ER])
        hw = sb("hw", [P, T, ER])
        expert = sb("expert", [P, T, E], I32)
        rank = sb("rank", [P, T, E])
        bias = sb("bias", [P, T, E])
        logit = sb("logit", [P, T, E])
        tied = sb("tied", [P, T, E])
        first = sb("first", [P, T, E])
        second = sb("second", [P, T, E])
        rest = sb("rest", [P, T, E])
        g1 = sb("g1", [P, T, E])
        top1 = sb("top1", [P, T])
        top2 = sb("top2", [P, T])
        pick1 = sb("pick1", [P, T])
        pick2 = sb("pick2", [P, T])
        gap = sb("gap", [P, T])
        egap = sb("egap", [P, T])
        esum = sb("esum", [P, T])
        w1 = sb("w1", [P, T])
        w2 = sb("w2", [P, T])
        top = sb("top", [P, T])
        shifted = sb("shifted", [P, T, E + 1])
        ex = sb("ex", [P, T, E + 1])
        den = sb("den", [P, T, 2])
        rden = sb("rden", [P, T, 2])
        prob = sb("prob", [P, T, E])
        adapted = sb("adapted", [P, T, E])
        weight = sb("weight", [P, T, E])
        wsum = sb("wsum", [P, T])
        wdiv = sb("wdiv", [P, T])
        rw = sb("rw", [P, T])
        g2 = sb("g2", [P, T, E])

        bank = [ctx.enter_context(nc.psum_tensor(f"bank{i}", [P, 512], F32)) for i in range(8)]
        F_BANK = [2, 3, 6, 7]
        G_BANK = 2
        MAIN_BANK = [4, 5, 6, 7]
        LAG = 3

        ld_a2, ld_wg, ld_wr, ld_a1, ld_b1, ld_b2, ld_b, ld_bthr, ld_itok = map(sem, (
            "ld_a2", "ld_wg", "ld_wr", "ld_a1", "ld_b1", "ld_b2", "ld_b", "ld_bthr", "ld_itok"))
        ld_w = [sem(f"ld_w{q}") for q in range(Q)]
        ld_x = [sem(f"ld_x{t}") for t in range(T)]
        ld_wb = [sem(f"ld_wb{c}") for c in range(2)]
        stored = sem("stored")
        a2_T, small_T, a1_T, x_T, wb_T, b2_T, hg_T, hw_T = map(sem, (
            "a2_T", "small_T", "a1_T", "x_T", "wb_T", "b2_T", "hg_T", "hw_T"))
        faux_mm, aux_mm, gaux_mm, f_mm, g_mm, y2_mm, main_mm = map(sem, (
            "faux_mm", "aux_mm", "gaux_mm", "f_mm", "g_mm", "y2_mm", "main_mm"))
        a2_sc, wg_sc, wr_hi, faux_hi, a1_hi, x_hi, aux_sc, wb_hi, gaux_sc, f_hi, g_hi, b2_hi, hg_sc, hg_hi, hw_hi = map(sem, (
            "a2_sc", "wg_sc", "wr_hi", "faux_hi", "a1_hi", "x_hi", "aux_sc", "wb_hi", "gaux_sc",
            "f_hi", "g_hi", "b2_hi", "hg_sc", "hg_hi", "hw_hi"))
        exp1, exp2 = sem("exp1"), sem("exp2")
        pad_set, wr_lo, faux_lo, a1_lo, x_lo, wb_lo, f_lo, g_lo, b2_lo, hg_lo, hw_lo = map(sem, (
            "pad_set", "wr_lo", "faux_lo", "a1_lo", "x_lo", "wb_lo", "f_lo", "g_lo", "b2_lo", "hg_lo", "hw_lo"))
        gap_set, hg_set, y2_set, shift_set, hw_set, out_set = map(sem, (
            "gap_set", "hg_set", "y2_set", "shift_set", "hw_set", "out_set"))
        dve_step = sem("dve_step")
        ident_zero, ident_set, iota_set, rank_set, w_hi, w_lo, pack_set, b1_hi, b1_lo, xb_set = map(sem, (
            "ident_zero", "ident_set", "iota_set", "rank_set", "w_hi", "w_lo", "pack_set", "b1_hi", "b1_lo", "xb_set"))

        block = ctx.enter_context(nc.Block())

        @block.sync
        def _(sp):
            sp.dma_start(A2_sb[:, :], A2_rows).then_inc(ld_a2, 16)
            for q in range(Q):
                sp.dma_start(W_sb[:, q, :], W_rows[:, q, :]).then_inc(ld_w[q], 16)
            for t in range(2, T):
                sp.dma_start(x_sb[:, t, :], x_tiles[t]).then_inc(ld_x[t], 16)
            for c in range(2):
                sp.dma_start(Wb_sb[:, 2 * c:2 * c + 2, :], Wb_rows[:, 2 * c:2 * c + 2, :]).then_inc(ld_wb[c], 16)
            sp.dma_start(B2_sb[:, :, :], B2_rows).then_inc(ld_b2, 16)
            for t in range(T):
                sp.wait_ge(out_set, t + 1)
                sp.dma_start(out_tiles[t], x_sb[:, t, :]).then_inc(stored, 16)
            sp.wait_ge(stored, 16 * T)

        @block.gpsimd
        def _(pool):
            nc.gpsimd.memset(ident[:, :], 0.0).then_inc(ident_zero, 1)
            pool.wait_ge(ident_zero, 1)
            nc.gpsimd.affine_select(out=ident[:, :], in_=ident[:, :], compare_op=ALU.not_equal, fill=1.0,
                                    base=0, pattern=[[-1, P]], channel_multiplier=1).then_inc(ident_set, 1)
            nc.gpsimd.iota(expert[:, :, :], pattern=[[0, T], [1, E]], base=0, channel_multiplier=0).then_inc(iota_set, 1)
            pool.wait_ge(iota_set, 1)
            nc.gpsimd.tensor_scalar(rank[:, :, :], expert[:, :, :], -1.0, float(E), ALU.mult, ALU.add).then_inc(rank_set, 1)
            for q in range(Q):
                pool.wait_ge(ld_w[q], 16)
                nc.gpsimd.tensor_copy(W_hi[:, q, :], W_sb[:, q, :]).then_inc(w_hi, 1)
                pool.wait_ge(w_hi, q + 1)
                nc.gpsimd.tensor_tensor(W_lo[:, q, :], W_sb[:, q, :], W_hi[:, q, :].bitcast(F32),
                                        ALU.subtract).then_inc(w_lo, 1)
            for ld, rows, pack in ((ld_b1, B1_sb, B1_pack), (ld_b2, B2_sb, B2_pack)):
                pool.wait_ge(ld, 16)
                nc.gpsimd.tensor_copy(pack[:, :, :].rearrange("p q (e r) -> p q e r", e=E),
                                      rows[:, :, :].rearrange("p e (q r) -> p q e r", q=Q)).then_inc(pack_set, 1)
            pool.wait_ge(pack_set, 1)
            nc.gpsimd.tensor_copy(B1_hi[:, :, :], B1_pack[:, :, :]).then_inc(b1_hi, 1)
            pool.wait_ge(b1_hi, 1)
            nc.gpsimd.tensor_tensor(B1_lo[:, :, :], B1_pack[:, :, :], B1_hi[:, :, :].bitcast(F32),
                                    ALU.subtract).then_inc(b1_lo, 1)
            pool.wait_ge(ld_b, 16)
            for t in range(T):
                pool.wait_ge(x_T, t + 1)
                nc.gpsimd.tensor_tensor(x_sb[:, t, :], x_sb[:, t, :], b_sb[:, :], ALU.add).then_inc(xb_set, 1)

        @block.scalar
        def _(act):
            act.dma_start(Wgt_sb[0:E, :], Wg).then_inc(ld_wg, 16)
            act.dma_start(Wgt_sb[E:E + 1, :], Wt).then_inc(ld_wg, 16)
            act.dma_start(Wr_sb[:, :], Wr).then_inc(ld_wr, 16)
            act.dma_start(A1_sb[:, :], A1_rows).then_inc(ld_a1, 16)
            for t in range(2):
                act.dma_start(x_sb[:, t, :], x_tiles[t]).then_inc(ld_x[t], 16)
            act.dma_start(itok_sb[:, :], itok.rearrange("(a t) -> a t", a=1).broadcast_to([P, T])).then_inc(ld_itok, 16)
            act.dma_start(bthr_sb[:, :], b_thr.rearrange("(a n) -> a n", a=1).broadcast_to([P, 1])).then_inc(ld_bthr, 16)
            act.dma_start(B1_sb[:, :, :], B1_rows).then_inc(ld_b1, 16)
            act.dma_start(b_sb[:, :], b_base.rearrange("(a n) -> a n", a=1).broadcast_to([P, D])).then_inc(ld_b, 16)

            def copy(dst, src):
                return nc.scalar.copy(dst, src)

            act.wait_ge(a2_T, 1)
            copy(M2auxT[:, :, 0:ER], bank[0][:, :].rearrange("p (q c) -> p q c", q=Q)).then_inc(a2_sc, 1)
            act.wait_ge(small_T, 1)
            copy(M2auxT[:, :, ER:NX], bank[1][:, 0:Q * (E + 1)].rearrange("p (q c) -> p q c", q=Q)).then_inc(wg_sc, 1)
            copy(aux_hi[:, :, C_R:C_X], bank[1][:, 64:64 + K * E].rearrange("p (k c) -> p k c", k=K)).then_inc(wr_hi, 1)
            for k in range(K):
                act.wait_ge(faux_mm, k + 1)
                copy(aux_hi[:, k, C_X:NAUX - 1], bank[4 + k][:, 0:NX]).then_inc(faux_hi, 1)
            act.wait_ge(a1_T, 1)
            copy(aux_hi[:, :, 0:ER], bank[0][:, :].rearrange("p (k c) -> p k c", k=K)).then_inc(a1_hi, 1)

            def x_part(t):
                act.wait_ge(x_T, t + 1)
                copy(xT_hi[:, :, t * P:(t + 1) * P],
                     bank[(t + 1) % 2][:, :].rearrange("p (k c) -> p k c", k=K)).then_inc(x_hi, 1)

            x_part(0)
            x_part(1)
            for t in range(T):
                act.wait_ge(aux_mm, t + 1)
                copy(xaux[:, t, :], bank[2 + t % 2][:, 0:NAUX - 1]).then_inc(aux_sc, 1)
                if t + 2 < T:
                    x_part(t + 2)
            for q in range(Q):
                act.wait_ge(wb_T, q + 1)
                copy(WbT_hi[:, q, :], bank[(q + 1) % 2][:, :]).then_inc(wb_hi, 1)
                if q == 1:
                    act.wait_ge(gaux_mm, 1)
                    copy(G_aux[:, :], bank[4][:, 0:NX]).then_inc(gaux_sc, 1)
            act.wait_ge(gap_set, 1)
            nc.scalar.activation(egap[:, :], gap[:, :], ACT.Exp).then_inc(exp1, 1)

            def f_part(k):
                act.wait_ge(f_mm, k + 1)
                copy(F_hi[:, k, :], bank[F_BANK[k]][:, :]).then_inc(f_hi, 1)

            f_part(0)
            act.wait_ge(b2_T, 1)
            copy(B2T_hi[:, :].rearrange("p (c q) -> p q c", q=Q),
                 bank[1][:, :].rearrange("p (q c) -> p q c", q=Q)).then_inc(b2_hi, 1)
            f_part(1)
            f_part(2)
            for h in range(2):
                half = slice(h * 4 * P, (h + 1) * 4 * P)
                act.wait_ge(hg_T, h + 1)
                copy(hgT[:, half], bank[h][:, :]).then_inc(hg_sc, 1)
                copy(hgT_hi[:, half], bank[h][:, :]).then_inc(hg_hi, 1)
            f_part(3)
            act.wait_ge(g_mm, 1)
            copy(G_hi[:, :], bank[G_BANK][:, :]).then_inc(g_hi, 1)
            act.wait_ge(shift_set, 2)
            nc.scalar.activation(ex[:, :, :], shifted[:, :, :], ACT.Exp).then_inc(exp2, 1)
            for h in range(2):
                act.wait_ge(hw_T, h + 1)
                copy(hwT_hi[:, h * 4 * P:(h + 1) * 4 * P], bank[h][:, :]).then_inc(hw_hi, 1)

        @block.tensor
        def _(pe):
            def product(dst, terms, first_in_bank=True, last=True):
                for n, (lhsT, rhs) in enumerate(terms):
                    mm = nc.tensor.matmul(dst, lhsT, rhs, start=first_in_bank and n == 0,
                                          stop=last and n == len(terms) - 1)
                return mm

            def three(a_hi, a_lo, b_hi, b_lo):
                return [(a_hi, b_hi), (a_hi, b_lo), (a_lo, b_hi)]

            pe.wait_ge(ident_set, 1)
            pe.wait_ge(ld_a2, 16)
            for q in range(Q):
                last = nc.tensor.transpose(bank[0][:, q * P:(q + 1) * P], A2_sb[:, q::Q], ident[:, :])
            last.then_inc(a2_T, 1)
            pe.wait_ge(ld_wg, 32)
            for q in range(Q):
                nc.tensor.transpose(bank[1][:, q * (E + 1):(q + 1) * (E + 1)], Wgt_sb[:, q::Q], ident[0:E + 1, 0:E + 1])
            pe.wait_ge(ld_wr, 16)
            for k in range(K):
                last = nc.tensor.transpose(bank[1][:, 64 + k * E:64 + (k + 1) * E], Wr_sb[:, k * P:(k + 1) * P],
                                           ident[0:E, 0:E])
            last.then_inc(small_T, 1)

            pe.wait_ge(a2_sc, 1)
            pe.wait_ge(wg_sc, 1)
            for q in range(Q):
                pe.wait_ge(ld_w[q], 16)
                for k in range(K):
                    last = nc.tensor.matmul(bank[4 + k][:, 0:NX], W_sb[:, q, k * P:(k + 1) * P], M2auxT[:, q, :],
                                            start=q == 0, stop=q == Q - 1)
                    if q == Q - 1:
                        last.then_inc(faux_mm, 1)

            pe.wait_ge(ld_a1, 16)
            for k in range(K):
                last = nc.tensor.transpose(bank[0][:, k * P:(k + 1) * P], A1_sb[:, k * P:(k + 1) * P], ident[:, :])
            last.then_inc(a1_T, 1)

            def transpose_x(t):
                pe.wait_ge(ld_x[t], 16)
                if t == 0:
                    pe.wait_ge(wr_lo, 1)
                elif t == 1:
                    pe.wait_ge(a1_lo, 1)
                else:
                    pe.wait_ge(x_lo, t - 1)
                for k in range(K):
                    last = nc.tensor.transpose(bank[(t + 1) % 2][:, k * P:(k + 1) * P],
                                               x_sb[:, t, k * P:(k + 1) * P], ident[:, :])
                last.then_inc(x_T, 1)

            def transpose_wb(q):
                pe.wait_ge(ld_wb[0], 16)
                pe.wait_ge(ld_wb[1], 16)
                if q < 2:
                    pe.wait_ge(x_lo, T - 1 + q)
                else:
                    pe.wait_ge(wb_lo, q - 1)
                for c in range(Q):
                    last = nc.tensor.transpose(bank[(q + 1) % 2][:, c * P:(c + 1) * P], Wb_sb[:, c, q::Q], ident[:, :])
                last.then_inc(wb_T, 1)

            transpose_x(0)
            transpose_x(1)
            pe.wait_ge(pad_set, 2)
            pe.wait_ge(wr_lo, 1)
            pe.wait_ge(faux_lo, K)
            pe.wait_ge(a1_lo, 1)
            for t in range(T):
                pe.wait_ge(x_lo, t + 1)
                if t >= 2:
                    pe.wait_ge(aux_sc, t - 1)
                tok = slice(t * P, (t + 1) * P)
                terms = []
                for k in range(K):
                    terms += three(xT_hi[:, k, tok], xT_lo[:, k, tok], aux_hi[:, k, :], aux_lo[:, k, :])
                product(bank[2 + t % 2][:, 0:NAUX], terms).then_inc(aux_mm, 1)
                if t + 2 < T:
                    transpose_x(t + 2)
                else:
                    transpose_wb(t + 2 - T)

            pe.wait_ge(pack_set, 1)
            product(bank[4][:, 0:NX], [(B1_pack[:, q, :], M2auxT[:, q, :]) for q in range(Q)]).then_inc(gaux_mm, 1)

            pe.wait_ge(w_lo, Q)
            for k in range(K):
                if F_BANK[k] == 2:
                    pe.wait_ge(aux_sc, T - 1)
                elif F_BANK[k] == 3:
                    pe.wait_ge(aux_sc, T)
                feat = slice(k * P, (k + 1) * P)
                for q in range(Q):
                    pe.wait_ge(wb_lo, q + 1)
                    last = product(bank[F_BANK[k]][:, :],
                                   three(W_hi[:, q, feat], W_lo[:, q, feat], WbT_hi[:, q, :], WbT_lo[:, q, :]),
                                   first_in_bank=q == 0, last=q == Q - 1)
                    if k == 0 and q < 2:
                        transpose_wb(q + 2)
                last.then_inc(f_mm, 1)
                if k == 0:
                    pe.wait_ge(pack_set, 2)
                    pe.wait_ge(wb_lo, 3)
                    for q in range(Q):
                        last = nc.tensor.transpose(bank[1][:, q * P:(q + 1) * P], B2_pack[:, q, :],
                                                   ident[:, :])
                    last.then_inc(b2_T, 1)
                if k == 2:
                    pe.wait_ge(hg_set, 1)
                    for h in range(2):
                        if h == 0:
                            pe.wait_ge(wb_lo, 4)
                        else:
                            pe.wait_ge(b2_lo, 1)
                        for i in range(4):
                            last = nc.tensor.transpose(bank[h][:, i * P:(i + 1) * P], hg[:, 4 * h + i, :], ident[:, :])
                        last.then_inc(hg_T, 1)

            pe.wait_ge(gaux_sc, 1)
            for j in range(T // PAIR):
                if j == 0:
                    pe.wait_ge(hg_sc, 1)
                if j == 1:
                    pe.wait_ge(faux_lo, 2)
                if j == 2:
                    pe.wait_ge(hg_sc, 2)
                if j >= 2:
                    pe.wait_ge(y2_set, j - 1)
                for i in range(PAIR):
                    t = PAIR * j + i
                    last = nc.tensor.matmul(bank[4 + j % 2][:, i * NX:(i + 1) * NX], hgT[:, t * P:(t + 1) * P],
                                            G_aux[:, :], start=True, stop=True)
                last.then_inc(y2_mm, 1)

            pe.wait_ge(b1_lo, 1)
            pe.wait_ge(f_lo, 1)
            terms = []
            for q in range(Q):
                terms += three(B1_hi[:, q, :], B1_lo[:, q, :], WbT_hi[:, q, :], WbT_lo[:, q, :])
            product(bank[G_BANK][:, :], terms).then_inc(g_mm, 1)

            def main_x(t):
                if t < 2:
                    pe.wait_ge(y2_set, 3 + t)
                elif t < 4:
                    pe.wait_ge(f_lo, 1 + t)
                else:
                    pe.wait_ge(out_set, t - 3)
                tok = slice(t * P, (t + 1) * P)
                for k in range(K):
                    if t == 0:
                        pe.wait_ge(f_lo, k + 1)
                    product(bank[MAIN_BANK[t % 4]][:, :],
                            three(xT_hi[:, k, tok], xT_lo[:, k, tok], F_hi[:, k, :], F_lo[:, k, :]),
                            first_in_bank=k == 0, last=False)

            def main_lora(t):
                if t == 0:
                    pe.wait_ge(g_lo, 1)
                    pe.wait_ge(hg_lo, 1)
                    pe.wait_ge(hw_lo, 1)
                if t == 4:
                    pe.wait_ge(hg_lo, 2)
                    pe.wait_ge(hw_lo, 2)
                tok = slice(t * P, (t + 1) * P)
                product(bank[MAIN_BANK[t % 4]][:, :],
                        three(hgT_hi[:, tok], hgT_lo[:, tok], G_hi[:, :], G_lo[:, :])
                        + three(hwT_hi[:, tok], hwT_lo[:, tok], B2T_hi[:, :], B2T_lo[:, :]),
                        first_in_bank=False).then_inc(main_mm, 1)

            for t in range(T + LAG):
                if t < T:
                    main_x(t)
                if t == LAG - 1:
                    pe.wait_ge(hw_set, 1)
                    for h in range(2):
                        pe.wait_ge(hg_lo, h + 1)
                        for i in range(4):
                            last = nc.tensor.transpose(bank[h][:, i * P:(i + 1) * P], hw[:, 4 * h + i, :], ident[:, :])
                        last.then_inc(hw_T, 1)
                if t >= LAG:
                    main_lora(t - LAG)

        @block.vector
        def _(dve):
            steps = [0]

            def link(ins):
                steps[0] += 1
                ins.then_inc(dve_step, 1)
                dve.wait_ge(dve_step, steps[0])

            def minus(lo, full, hi):
                return nc.vector.tensor_tensor(lo, full, hi.bitcast(F32), ALU.subtract)

            def over_experts(v):
                return v.unsqueeze(2).broadcast_to([P, T, E])

            nc.vector.memset(aux_hi[:, :, NAUX - 1:NAUX].bitcast(F32), 0.0).then_inc(pad_set, 1)
            nc.vector.memset(aux_lo[:, :, NAUX - 1:NAUX].bitcast(F32), 0.0).then_inc(pad_set, 1)

            dve.wait_ge(wr_hi, 1)
            minus(aux_lo[:, :, C_R:C_X], bank[1][:, 64:64 + K * E].rearrange("p (k c) -> p k c", k=K),
                  aux_hi[:, :, C_R:C_X]).then_inc(wr_lo, 1)
            dve.wait_ge(ld_itok, 16)
            dve.wait_ge(iota_set, 1)
            link(nc.vector.tensor_tensor(bias[:, :, :], over_experts(itok_sb[:, :]), expert[:, :, :], ALU.is_equal))
            for k in range(K):
                dve.wait_ge(faux_hi, k + 1)
                minus(aux_lo[:, k, C_X:NAUX - 1], bank[4 + k][:, 0:NX], aux_hi[:, k, C_X:NAUX - 1]).then_inc(faux_lo, 1)
            dve.wait_ge(a1_hi, 1)
            minus(aux_lo[:, :, 0:ER], bank[0][:, :].rearrange("p (k c) -> p k c", k=K),
                  aux_hi[:, :, 0:ER]).then_inc(a1_lo, 1)
            for t in range(T):
                dve.wait_ge(x_hi, t + 1)
                minus(xT_lo[:, :, t * P:(t + 1) * P], bank[(t + 1) % 2][:, :].rearrange("p (k c) -> p k c", k=K),
                      xT_hi[:, :, t * P:(t + 1) * P]).then_inc(x_lo, 1)
            for q in range(Q):
                dve.wait_ge(wb_hi, q + 1)
                minus(WbT_lo[:, q, :], bank[(q + 1) % 2][:, :], WbT_hi[:, q, :]).then_inc(wb_lo, 1)

            dve.wait_ge(aux_sc, T)
            link(nc.vector.scalar_tensor_tensor(logit[:, :, :], bias[:, :, :], LANG_BIAS, xaux[:, :, C_R:C_X],
                                                ALU.mult, ALU.add))
            link(nc.vector.tensor_reduce(top1[:, :], logit[:, :, :], AX.X, ALU.max))
            link(nc.vector.tensor_tensor(tied[:, :, :], logit[:, :, :], over_experts(top1[:, :]), ALU.is_equal))
            dve.wait_ge(rank_set, 1)
            link(nc.vector.tensor_tensor(tied[:, :, :], tied[:, :, :], rank[:, :, :], ALU.mult))
            link(nc.vector.tensor_reduce(pick1[:, :], tied[:, :, :], AX.X, ALU.max))
            link(nc.vector.tensor_tensor(first[:, :, :], rank[:, :, :], over_experts(pick1[:, :]), ALU.is_equal))
            link(nc.vector.scalar_tensor_tensor(rest[:, :, :], first[:, :, :], MASKED, logit[:, :, :],
                                                ALU.mult, ALU.add))
            link(nc.vector.tensor_reduce(top2[:, :], rest[:, :, :], AX.X, ALU.max))
            nc.vector.tensor_tensor(gap[:, :], top2[:, :], top1[:, :], ALU.subtract).then_inc(gap_set, 1)
            link(nc.vector.tensor_tensor(tied[:, :, :], rest[:, :, :], over_experts(top2[:, :]), ALU.is_equal))
            link(nc.vector.tensor_tensor(tied[:, :, :], tied[:, :, :], rank[:, :, :], ALU.mult))
            link(nc.vector.tensor_reduce(pick2[:, :], tied[:, :, :], AX.X, ALU.max))
            link(nc.vector.tensor_tensor(second[:, :, :], rank[:, :, :], over_experts(pick2[:, :]), ALU.is_equal))
            dve.wait_ge(exp1, 1)
            link(nc.vector.tensor_scalar(esum[:, :], egap[:, :], 1.0, 1.0 / SCALING, ALU.add, ALU.mult))
            link(nc.vector.reciprocal(w1[:, :], esum[:, :]))
            link(nc.vector.tensor_tensor(w2[:, :], w1[:, :], egap[:, :], ALU.mult))
            link(nc.vector.tensor_tensor(first[:, :, :], first[:, :, :], over_experts(w1[:, :]), ALU.mult))
            link(nc.vector.tensor_tensor(second[:, :, :], second[:, :, :], over_experts(w2[:, :]), ALU.mult))
            link(nc.vector.tensor_tensor(g1[:, :, :], first[:, :, :], second[:, :, :], ALU.add))
            nc.vector.tensor_tensor(hg[:, :, :].rearrange("p t (e r) -> p t e r", e=E),
                                    xaux[:, :, 0:ER].rearrange("p t (e r) -> p t e r", e=E),
                                    g1[:, :, :].unsqueeze(3).broadcast_to([P, T, E, R]), ALU.mult).then_inc(hg_set, 1)

            def f_part(k):
                dve.wait_ge(f_hi, k + 1)
                minus(F_lo[:, k, :], bank[F_BANK[k]][:, :], F_hi[:, k, :]).then_inc(f_lo, 1)

            f_part(0)
            dve.wait_ge(b2_hi, 1)
            minus(B2T_lo[:, :].rearrange("p (c q) -> p q c", q=Q), bank[1][:, :].rearrange("p (q c) -> p q c", q=Q),
                  B2T_hi[:, :].rearrange("p (c q) -> p q c", q=Q)).then_inc(b2_lo, 1)
            f_part(1)
            f_part(2)
            for h in range(2):
                half = slice(h * 4 * P, (h + 1) * 4 * P)
                dve.wait_ge(hg_hi, h + 1)
                minus(hgT_lo[:, half], bank[h][:, :], hgT_hi[:, half]).then_inc(hg_lo, 1)
            f_part(3)

            for j in range(T // PAIR):
                dve.wait_ge(y2_mm, j + 1)
                pair = slice(PAIR * j, PAIR * (j + 1))
                nc.vector.tensor_tensor(y2[:, pair, :],
                                        bank[4 + j % 2][:, 0:PAIR * NX].rearrange("p (i c) -> p i c", i=PAIR),
                                        xaux[:, pair, C_X:C_X + NX], ALU.add).then_inc(y2_set, 1)
            dve.wait_ge(y2_set, T // PAIR)
            link(nc.vector.tensor_reduce(top[:, :], y2[:, :, ER:ER + E], AX.X, ALU.max))
            dve.wait_ge(ld_bthr, 16)
            nc.vector.tensor_scalar(shifted[:, :, E], y2[:, :, ER + E], -1.0, bthr_sb[:, 0:1],
                                    ALU.mult, ALU.subtract).then_inc(shift_set, 1)
            nc.vector.tensor_tensor(shifted[:, :, 0:E], y2[:, :, ER:ER + E], over_experts(top[:, :]),
                                    ALU.subtract).then_inc(shift_set, 1)
            dve.wait_ge(g_hi, 1)
            minus(G_lo[:, :], bank[G_BANK][:, :], G_hi[:, :]).then_inc(g_lo, 1)
            dve.wait_ge(exp2, 1)
            link(nc.vector.tensor_reduce(den[:, :, 0], ex[:, :, 0:E], AX.X, ALU.add))
            link(nc.vector.tensor_scalar(den[:, :, 1], ex[:, :, E], 1.0, None, ALU.add))
            link(nc.vector.reciprocal(rden[:, :, :], den[:, :, :]))
            link(nc.vector.tensor_tensor(prob[:, :, :], ex[:, :, 0:E], over_experts(rden[:, :, 0]), ALU.mult))
            link(nc.vector.scalar_tensor_tensor(adapted[:, :, :], over_experts(rden[:, :, 1]), -MAX_THRESHOLD,
                                                prob[:, :, :], ALU.mult, ALU.add))
            link(nc.vector.tensor_scalar(weight[:, :, :], adapted[:, :, :], 0.0, None, ALU.max))
            link(nc.vector.tensor_reduce(wsum[:, :], weight[:, :, :], AX.X, ALU.add))
            link(nc.vector.scalar_tensor_tensor(wdiv[:, :], wsum[:, :], 0.0, wsum[:, :], ALU.is_equal, ALU.add))
            link(nc.vector.reciprocal(rw[:, :], wdiv[:, :]))
            link(nc.vector.scalar_tensor_tensor(g2[:, :, :], weight[:, :, :], SCALING, over_experts(rw[:, :]),
                                                ALU.mult, ALU.mult))
            nc.vector.tensor_tensor(hw[:, :, :].rearrange("p t (e r) -> p t e r", e=E),
                                    y2[:, :, 0:ER].rearrange("p t (e r) -> p t e r", e=E),
                                    g2[:, :, :].unsqueeze(3).broadcast_to([P, T, E, R]), ALU.mult).then_inc(hw_set, 1)
            for h in range(2):
                half = slice(h * 4 * P, (h + 1) * 4 * P)
                dve.wait_ge(hw_hi, h + 1)
                minus(hwT_lo[:, half], bank[h][:, :], hwT_hi[:, half]).then_inc(hw_lo, 1)
            for t in range(T):
                dve.wait_ge(main_mm, t + 1)
                dve.wait_ge(xb_set, t + 1)
                nc.vector.tensor_tensor(x_sb[:, t, :], bank[MAIN_BANK[t % 4]][:, :], x_sb[:, t, :],
                                        ALU.add).then_inc(out_set, 1)


_INS = ['x', 'itok_B_0_7', 'L0_cond_W', 'L0_cond_Wr', 'L0_cond_A', 'L0_cond_B', 'L0_ffn_W_base', 'L0_ffn_b_base',
        'L0_ffn_W_gate', 'L0_ffn_W_thr', 'L0_ffn_b_thr', 'L0_ffn_A', 'L0_ffn_B']
_OUTS = [((8, 128, 512), 'float32')]


def kernel(**inputs):
    import numpy as _np
    import concourse.bacc as _bacc
    from concourse import mybir as _mybir
    from concourse.bass_utils import run_bass_kernel_spmd as _run

    nc = _bacc.Bacc("TRN2", target_bir_lowering=False, num_devices=1)
    arrays, args = {}, []
    for name in _INS:
        a = _np.ascontiguousarray(inputs[name])
        arrays[f"in_{name}_dram"] = a
        args.append(nc.dram_tensor(f"in_{name}_dram", a.shape, _mybir.dt.from_np(a.dtype), kind="ExternalInput").ap())
    for i, (shape, dtype) in enumerate(_OUTS):
        dt = _mybir.dt.from_np(_np.dtype(dtype))
        args.append(nc.dram_tensor(f"out_{i}_dram", shape, dt, kind="ExternalOutput").ap())
    adaln_ffn_kernel(nc, *args)
    r = _run(nc, [arrays], core_ids=[0])
    return r.results[0]["out_0_dram"]
```

```python
from contextlib import ExitStack

import concourse.bass as bass
from concourse import mybir

ALU = mybir.AluOpType
ACT = mybir.ActivationFunctionType
AX = mybir.AxisListType
F32 = mybir.dt.float32
F32R = mybir.dt.float32r
BF16 = mybir.dt.bfloat16
I32 = mybir.dt.int32

P = 128
LANG_BIAS = 5.0
SCALING = 2.0
MAX_THRESHOLD = 0.125
MASKED = -3.0e38


def adaln_ffn_kernel(nc, xT, itok, W, WbT, narrow1T, narrow2T, B1, B2T, b_base, b_thr, out):
    CHUNKS, _, K, CT = xT.shape
    _, Q, D = W.shape
    O = WbT.shape[2]
    ER = B1.shape[2]
    N1, N2 = narrow1T.shape[2], narrow2T.shape[2]
    E = N1 - ER
    R = ER // E
    T = CHUNKS * CT // P
    TC = CT // P
    GROUP = 4
    GROUPS = T // GROUP
    PAIR = 2
    NX = N1 + N2
    NXE = NX + NX % 2
    assert ER == P and out.shape[0] == T * P

    out_tiles = out.rearrange("(t p) o -> t p o", p=P)

    ctx = ExitStack()
    with ctx:
        def sb(name, shape, dt=F32):
            return ctx.enter_context(nc.sbuf_tensor(name, shape, dt))

        def sem(name):
            return ctx.enter_context(nc.semaphore(name))

        xT_sb = sb("xT_sb", [P, K, T * P])
        W_sb = sb("W_sb", [P, Q, D])
        WbT_sb = sb("WbT_sb", [P, Q, O])
        narrow1_sb = sb("narrow1_sb", [P, K, N1])
        narrow2_sb = sb("narrow2_sb", [P, Q, N2])
        B1_sb = sb("B1_sb", [P, Q, ER])
        B2T_sb = sb("B2T_sb", [P, O])
        b_sb = sb("b_sb", [P, O])
        bthr_sb = sb("bthr_sb", [P, 1])
        itok_sb = sb("itok_sb", [P, T], I32)

        ident = sb("ident", [P, P])
        ident_bf = sb("ident_bf", [P, P], BF16)
        xT_hi = sb("xT_hi", [P, K, T * P], F32R)
        xT_lo = sb("xT_lo", [P, K, T * P], F32R)
        W_hi = sb("W_hi", [P, Q, D], F32R)
        W_lo = sb("W_lo", [P, Q, D], F32R)
        WbT_hi = sb("WbT_hi", [P, Q, O], F32R)
        WbT_lo = sb("WbT_lo", [P, Q, O], F32R)
        narrow_hi = sb("narrow_hi", [P, K, NXE], F32R)
        narrow_lo = sb("narrow_lo", [P, K, NXE], F32R)
        B1_hi = sb("B1_hi", [P, Q, ER], F32R)
        B1_lo = sb("B1_lo", [P, Q, ER], F32R)
        F_hi = sb("F_hi", [P, K, O], F32R)
        F_lo = sb("F_lo", [P, K, O], F32R)
        G_narrow = sb("G_narrow", [P, N2])
        G_hi = sb("G_hi", [P, O], F32R)
        G_lo = sb("G_lo", [P, O], F32R)
        B2T_hi = sb("B2T_hi", [P, O], F32R)
        B2T_lo = sb("B2T_lo", [P, O], F32R)
        hgT = sb("hgT", [P, T * P])
        hgT_hi = sb("hgT_hi", [P, T * P], F32R)
        hgT_lo = sb("hgT_lo", [P, T * P], F32R)
        hwT_hi = sb("hwT_hi", [P, T * P], F32R)
        hwT_lo = sb("hwT_lo", [P, T * P], F32R)

        xn = sb("xn", [P, T, NX])
        y2 = sb("y2", [P, T, N2])
        hg = sb("hg", [P, T, ER])
        hw = sb("hw", [P, T, ER])
        expert = sb("expert", [P, T, E], I32)
        rank = sb("rank", [P, T, E])
        spoken = sb("spoken", [P, T, E])
        logit = sb("logit", [P, T, E])
        tied1, first, rest, tied2, second = (sb(n, [P, T, E]) for n in ("tied1", "first", "rest", "tied2", "second"))
        ranked1, ranked2, gate1, gate2, g1 = (sb(n, [P, T, E]) for n in ("ranked1", "ranked2", "gate1", "gate2", "g1"))
        top1, top2, pick1, pick2 = (sb(n, [P, T]) for n in ("top1", "top2", "pick1", "pick2"))
        gap, egap, esum, w1, w2 = (sb(n, [P, T]) for n in ("gap", "egap", "esum", "w1", "w2"))
        top = sb("top", [P, T])
        shifted = sb("shifted", [P, T, E + 1])
        ex = sb("ex", [P, T, E + 1])
        den = sb("den", [P, T, 2])
        rden = sb("rden", [P, T, 2])
        prob, adapted, weight, g2 = (sb(n, [P, T, E]) for n in ("prob", "adapted", "weight", "g2"))
        wsum, wdiv, rw = (sb(n, [P, T]) for n in ("wsum", "wdiv", "rw"))
        out_sb = sb("out_sb", [P, T, O])

        bank = [ctx.enter_context(nc.psum_tensor(f"bank{i}", [P, 512], F32)) for i in range(8)]
        FN_BANK = [0, 1, 2, 3]
        F_BANK = [4, 5, 6, 7]
        XN_BANK = [0, 1]
        G_BANK, GN_BANK = 2, 3
        TR_BANK = [2, 3]
        Y2_BANK = [0, 1]
        OUT_BANK = [4, 5, 6, 7, 0, 1]
        RING = len(OUT_BANK)

        ld_n1, ld_n2, ld_b1, ld_b2, ld_b, ld_bthr, ld_itok = map(sem, (
            "ld_n1", "ld_n2", "ld_b1", "ld_b2", "ld_b", "ld_bthr", "ld_itok"))
        ld_w = [sem(f"ld_w{q}") for q in range(Q)]
        ld_wb = [sem(f"ld_wb{q}") for q in range(Q)]
        ld_x = [sem(f"ld_x{c}") for c in range(CHUNKS)]
        stored = sem("stored")
        fn_mm, f_mm, xn_mm, gn_mm, g_mm, y2_mm, out_mm, hg_T, hw_T = map(sem, (
            "fn_mm", "f_mm", "xn_mm", "gn_mm", "g_mm", "y2_mm", "out_mm", "hg_T", "hw_T"))
        w_hi, wb_hi, n1_hi, x_hi, fn_hi, xn_sc, f_hi, gn_sc, g_hi, hg_sc, hg_hi, hw_hi, exp1, exp2 = map(sem, (
            "w_hi", "wb_hi", "n1_hi", "x_hi", "fn_hi", "xn_sc", "f_hi", "gn_sc", "g_hi", "hg_sc", "hg_hi",
            "hw_hi", "exp1", "exp2"))
        pad_set, w_lo, wb_lo, n1_lo, x_lo, fn_lo, f_lo, g_lo, hg_lo, hw_lo = map(sem, (
            "pad_set", "w_lo", "wb_lo", "n1_lo", "x_lo", "fn_lo", "f_lo", "g_lo", "hg_lo", "hw_lo"))
        gap_set, hg_set, y2_set, shift_set, hw_set, out_set, step_done = map(sem, (
            "gap_set", "hg_set", "y2_set", "shift_set", "hw_set", "out_set", "step_done"))
        ident_zero, ident_set, ident_bf_set, iota_set, rank_set, b1_hi, b1_lo, b2_hi, b2_lo = map(sem, (
            "ident_zero", "ident_set", "ident_bf_set", "iota_set", "rank_set", "b1_hi", "b1_lo", "b2_hi", "b2_lo"))

        def tok(t):
            return slice(t * P, (t + 1) * P)

        def group_tok(g):
            return slice(g * GROUP * P, (g + 1) * GROUP * P)

        def chunk_tok(c):
            return slice(c * CT, (c + 1) * CT)

        block = ctx.enter_context(nc.Block())

        @block.sync
        def _(sp):
            sp.dma_start(narrow2_sb[:, :, :], narrow2T).then_inc(ld_n2, 16)
            for q in range(Q):
                sp.dma_start(W_sb[:, q, :], W[:, q, :]).then_inc(ld_w[q], 16)
                sp.dma_start(WbT_sb[:, q, :], WbT[:, q, :]).then_inc(ld_wb[q], 16)
            sp.dma_start(xT_sb[:, :, chunk_tok(0)], xT[0]).then_inc(ld_x[0], 16)
            sp.dma_start(narrow1_sb[:, :, :], narrow1T).then_inc(ld_n1, 16)
            for c in range(1, CHUNKS):
                sp.dma_start(xT_sb[:, :, chunk_tok(c)], xT[c]).then_inc(ld_x[c], 16)
            sp.dma_start(B1_sb[:, :, :], B1).then_inc(ld_b1, 16)
            sp.dma_start(itok_sb[:, :], itok.broadcast_to([P, T])).then_inc(ld_itok, 16)
            sp.dma_start(bthr_sb[:, :], b_thr.broadcast_to([P, 1])).then_inc(ld_bthr, 16)
            sp.dma_start(B2T_sb[:, :], B2T).then_inc(ld_b2, 16)
            sp.dma_start(b_sb[:, :], b_base.broadcast_to([P, O])).then_inc(ld_b, 16)
            for t in range(T):
                sp.wait_ge(out_set, t + 1)
                sp.dma_start(out_tiles[t], out_sb[:, t, :]).then_inc(stored, 16)
            sp.wait_ge(stored, 16 * T)

        @block.gpsimd
        def _(pool):
            nc.gpsimd.memset(ident[:, :], 0.0).then_inc(ident_zero, 1)
            pool.wait_ge(ident_zero, 1)
            nc.gpsimd.affine_select(out=ident[:, :], in_=ident[:, :], compare_op=ALU.not_equal, fill=1.0,
                                    base=0, pattern=[[-1, P]], channel_multiplier=1).then_inc(ident_set, 1)
            pool.wait_ge(ident_set, 1)
            nc.gpsimd.tensor_copy(ident_bf[:, :], ident[:, :]).then_inc(ident_bf_set, 1)
            nc.gpsimd.iota(expert[:, :, :], pattern=[[0, T], [1, E]], base=0, channel_multiplier=0).then_inc(iota_set, 1)
            pool.wait_ge(iota_set, 1)
            nc.gpsimd.tensor_scalar(rank[:, :, :], expert[:, :, :], -1.0, float(E), ALU.mult, ALU.add).then_inc(rank_set, 1)
            for ld, whole, hi, lo, hi_set, lo_set in (
                    (ld_b1, B1_sb[:, :, :], B1_hi[:, :, :], B1_lo[:, :, :], b1_hi, b1_lo),
                    (ld_b2, B2T_sb[:, :], B2T_hi[:, :], B2T_lo[:, :], b2_hi, b2_lo)):
                pool.wait_ge(ld, 16)
                nc.gpsimd.tensor_copy(hi, whole).then_inc(hi_set, 1)
                pool.wait_ge(hi_set, 1)
                nc.gpsimd.tensor_tensor(lo, whole, hi.bitcast(F32), ALU.subtract).then_inc(lo_set, 1)

        @block.scalar
        def _(act):
            nc.scalar.preload_act_table(ACT.Exp)

            def copy(dst, src):
                return nc.scalar.copy(dst, src)

            for q in range(Q):
                act.wait_ge(ld_w[q], 16)
                copy(W_hi[:, q, :], W_sb[:, q, :]).then_inc(w_hi, 1)
                act.wait_ge(ld_wb[q], 16)
                copy(WbT_hi[:, q, :], WbT_sb[:, q, :]).then_inc(wb_hi, 1)
            for c in range(CHUNKS):
                act.wait_ge(ld_x[c], 16)
                copy(xT_hi[:, :, chunk_tok(c)], xT_sb[:, :, chunk_tok(c)]).then_inc(x_hi, 1)
                if c == 0:
                    act.wait_ge(ld_n1, 16)
                    copy(narrow_hi[:, :, 0:N1], narrow1_sb[:, :, :]).then_inc(n1_hi, 1)
            for k in range(K):
                act.wait_ge(fn_mm, k + 1)
                copy(narrow_hi[:, k, N1:NX], bank[FN_BANK[k]][:, 0:N2]).then_inc(fn_hi, 1)

            def xn_copy(t):
                act.wait_ge(xn_mm, t + 1)
                copy(xn[:, t, :], bank[XN_BANK[t % 2]][:, 0:NX]).then_inc(xn_sc, 1)

            def hgT_copy(g):
                act.wait_ge(hg_T, g + 1)
                copy(hgT[:, group_tok(g)], bank[TR_BANK[g]][:, :]).then_inc(hg_sc, 1)
                copy(hgT_hi[:, group_tok(g)], bank[TR_BANK[g]][:, :]).then_inc(hg_hi, 1)

            def exp_gap(g):
                act.wait_ge(gap_set, g + 1)
                nc.scalar.activation(egap[:, g * GROUP:(g + 1) * GROUP], gap[:, g * GROUP:(g + 1) * GROUP],
                                     ACT.Exp).then_inc(exp1, 1)

            def exp_shifted(g):
                act.wait_ge(shift_set, 2 * (g + 1))
                nc.scalar.activation(ex[:, g * GROUP:(g + 1) * GROUP, :], shifted[:, g * GROUP:(g + 1) * GROUP, :],
                                     ACT.Exp).then_inc(exp2, 1)

            def hwT_copy(g):
                act.wait_ge(hw_T, g + 1)
                copy(hwT_hi[:, group_tok(g)], bank[TR_BANK[g]][:, :]).then_inc(hw_hi, 1)

            for t in range(GROUP):
                act.wait_ge(f_mm, t + 1)
                copy(F_hi[:, t, :], bank[F_BANK[t]][:, :]).then_inc(f_hi, 1)
                xn_copy(t)
            act.wait_ge(gn_mm, 1)
            copy(G_narrow[:, :], bank[GN_BANK][:, 0:N2]).then_inc(gn_sc, 1)
            exp_gap(0)
            act.wait_ge(g_mm, 1)
            copy(G_hi[:, :], bank[G_BANK][:, :]).then_inc(g_hi, 1)
            for t in range(GROUP, T):
                xn_copy(t)
            hgT_copy(0)
            exp_gap(1)
            hgT_copy(1)
            exp_shifted(0)
            hwT_copy(0)
            exp_shifted(1)
            hwT_copy(1)

        @block.tensor
        def _(pe):
            def product(dst, terms, first=True, last=True):
                for n, (lhsT, rhs) in enumerate(terms):
                    mm = nc.tensor.matmul(dst, lhsT, rhs, start=first and n == 0, stop=last and n == len(terms) - 1)
                return mm

            def three(a_hi, a_lo, b_hi, b_lo):
                return [(a_hi, b_hi), (a_hi, b_lo), (a_lo, b_hi)]

            pe.wait_ge(ld_n2, 16)
            for q in range(Q):
                pe.wait_ge(ld_w[q], 16)
                for k in range(K):
                    mm = nc.tensor.matmul(bank[FN_BANK[k]][:, 0:N2], W_sb[:, q, k * P:(k + 1) * P],
                                          narrow2_sb[:, q, :], start=q == 0, stop=q == Q - 1)
                    if q == Q - 1:
                        mm.then_inc(fn_mm, 1)
                if q == 0:
                    pe.wait_ge(ident_bf_set, 1)
                pe.wait_ge(w_lo, q + 1)
                pe.wait_ge(wb_lo, q + 1)
                for k in range(K):
                    feat = slice(k * P, (k + 1) * P)
                    mm = product(bank[F_BANK[k]][:, :],
                                 three(W_hi[:, q, feat], W_lo[:, q, feat], WbT_hi[:, q, :], WbT_lo[:, q, :]),
                                 first=q == 0, last=False)
                    if q == Q - 1:
                        mm = nc.tensor.matmul(bank[F_BANK[k]][:, feat], ident_bf[:, :], ident_bf[:, :],
                                              start=False, stop=True)
                        mm.then_inc(f_mm, 1)

            def x_narrow(t):
                pe.wait_ge(x_lo, t // TC + 1)
                if t == 0:
                    pe.wait_ge(pad_set, 2)
                    pe.wait_ge(n1_lo, 1)
                    pe.wait_ge(fn_lo, K)
                if t >= 2:
                    pe.wait_ge(xn_sc, t - 1)
                terms = []
                for k in range(K):
                    terms += three(xT_hi[:, k, tok(t)], xT_lo[:, k, tok(t)], narrow_hi[:, k, :], narrow_lo[:, k, :])
                product(bank[XN_BANK[t % 2]][:, 0:NXE], terms).then_inc(xn_mm, 1)

            def transpose_group(h, g):
                for i in range(GROUP):
                    last = nc.tensor.transpose(bank[TR_BANK[g]][:, i * P:(i + 1) * P], h[:, g * GROUP + i, :], ident[:, :])
                return last

            def transpose_hg(g):
                pe.wait_ge(hg_set, g + 1)
                if g == 0:
                    pe.wait_ge(ident_set, 1)
                    pe.wait_ge(g_lo, 1)
                else:
                    pe.wait_ge(gn_sc, 1)
                transpose_group(hg, g).then_inc(hg_T, 1)

            def transpose_hw(g):
                pe.wait_ge(hw_set, g + 1)
                pe.wait_ge(hg_lo, g + 1)
                transpose_group(hw, g).then_inc(hw_T, 1)

            def y2_group(g):
                pe.wait_ge(gn_sc, 1)
                pe.wait_ge(hg_sc, g + 1)
                for j in range(g * GROUP // PAIR, (g + 1) * GROUP // PAIR):
                    if j < 2:
                        pe.wait_ge(xn_sc, T - 1 + j)
                    else:
                        pe.wait_ge(y2_set, j - 1)
                    for i in range(PAIR):
                        last = nc.tensor.matmul(bank[Y2_BANK[j % 2]][:, i * N2:(i + 1) * N2],
                                                hgT[:, tok(PAIR * j + i)], G_narrow[:, :], start=True, stop=True)
                    last.then_inc(y2_mm, 1)

            def out_x(t):
                if t < K:
                    pe.wait_ge(f_lo, K)
                elif t < RING:
                    pe.wait_ge(y2_set, T // PAIR - RING + 1 + t)
                else:
                    pe.wait_ge(out_set, t - RING + 1)
                terms = []
                for k in range(K):
                    terms += three(xT_hi[:, k, tok(t)], xT_lo[:, k, tok(t)], F_hi[:, k, :], F_lo[:, k, :])
                product(bank[OUT_BANK[t % RING]][:, :], terms, last=False)

            def out_lora(t):
                if t == 0:
                    pe.wait_ge(b2_lo, 1)
                pe.wait_ge(hw_lo, t // GROUP + 1)
                product(bank[OUT_BANK[t % RING]][:, :],
                        three(hgT_hi[:, tok(t)], hgT_lo[:, tok(t)], G_hi[:, :], G_lo[:, :])
                        + three(hwT_hi[:, tok(t)], hwT_lo[:, tok(t)], B2T_hi[:, :], B2T_lo[:, :]),
                        first=False).then_inc(out_mm, 1)

            for t in range(GROUP):
                x_narrow(t)
            pe.wait_ge(ld_b1, 16)
            product(bank[GN_BANK][:, 0:N2], [(B1_sb[:, q, :], narrow2_sb[:, q, :]) for q in range(Q)]).then_inc(gn_mm, 1)
            pe.wait_ge(b1_lo, 1)
            terms = []
            for q in range(Q):
                terms += three(B1_hi[:, q, :], B1_lo[:, q, :], WbT_hi[:, q, :], WbT_lo[:, q, :])
            product(bank[G_BANK][:, :], terms).then_inc(g_mm, 1)
            for t in range(GROUP, T):
                x_narrow(t)
            transpose_hg(0)
            out_x(0)
            y2_group(0)
            out_x(1)
            transpose_hg(1)
            out_x(2)
            y2_group(1)
            transpose_hw(0)
            out_x(3)
            out_lora(0)
            out_x(4)
            out_lora(1)
            transpose_hw(1)
            for t in range(5, T):
                out_x(t)
                out_lora(t - 3)
            for t in range(T - 3, T):
                out_lora(t)

        @block.vector
        def _(dve):
            steps = [0]

            def link(ins):
                steps[0] += 1
                ins.then_inc(step_done, 1)
                dve.wait_ge(step_done, steps[0])

            def minus(lo, whole, hi):
                return nc.vector.tensor_tensor(lo, whole, hi.bitcast(F32), ALU.subtract)

            def over_experts(v):
                return v.unsqueeze(2).broadcast_to([P, v.shape[1], E])

            def over_rank(v):
                return v.unsqueeze(3).broadcast_to([P, v.shape[1], E, R])

            nc.vector.memset(narrow_hi[:, :, NX:NXE].bitcast(F32), 0.0).then_inc(pad_set, 1)
            nc.vector.memset(narrow_lo[:, :, NX:NXE].bitcast(F32), 0.0).then_inc(pad_set, 1)

            for q in range(Q):
                dve.wait_ge(w_hi, q + 1)
                minus(W_lo[:, q, :], W_sb[:, q, :], W_hi[:, q, :]).then_inc(w_lo, 1)
                dve.wait_ge(wb_hi, q + 1)
                minus(WbT_lo[:, q, :], WbT_sb[:, q, :], WbT_hi[:, q, :]).then_inc(wb_lo, 1)
            for c in range(CHUNKS):
                dve.wait_ge(x_hi, c + 1)
                minus(xT_lo[:, :, chunk_tok(c)], xT_sb[:, :, chunk_tok(c)], xT_hi[:, :, chunk_tok(c)]).then_inc(x_lo, 1)
                if c == 0:
                    dve.wait_ge(n1_hi, 1)
                    minus(narrow_lo[:, :, 0:N1], narrow1_sb[:, :, :], narrow_hi[:, :, 0:N1]).then_inc(n1_lo, 1)
            for k in range(K):
                dve.wait_ge(fn_hi, k + 1)
                minus(narrow_lo[:, k, N1:NX], bank[FN_BANK[k]][:, 0:N2], narrow_hi[:, k, N1:NX]).then_inc(fn_lo, 1)
            for k in range(K):
                dve.wait_ge(f_hi, k + 1)
                minus(F_lo[:, k, :], bank[F_BANK[k]][:, :], F_hi[:, k, :]).then_inc(f_lo, 1)
            dve.wait_ge(ld_itok, 16)
            dve.wait_ge(iota_set, 1)
            link(nc.vector.tensor_tensor(spoken[:, :, :], over_experts(itok_sb[:, :]), expert[:, :, :], ALU.is_equal))

            def layer1_gates(g):
                s = slice(g * GROUP, (g + 1) * GROUP)
                dve.wait_ge(xn_sc, (g + 1) * GROUP)
                link(nc.vector.scalar_tensor_tensor(logit[:, s, :], spoken[:, s, :], LANG_BIAS, xn[:, s, ER:N1],
                                                    ALU.mult, ALU.add))
                link(nc.vector.tensor_reduce(top1[:, s], logit[:, s, :], AX.X, ALU.max))
                link(nc.vector.tensor_tensor(tied1[:, s, :], logit[:, s, :], over_experts(top1[:, s]), ALU.is_equal))
                if g == 0:
                    dve.wait_ge(rank_set, 1)
                link(nc.vector.tensor_tensor(ranked1[:, s, :], tied1[:, s, :], rank[:, s, :], ALU.mult))
                link(nc.vector.tensor_reduce(pick1[:, s], ranked1[:, s, :], AX.X, ALU.max))
                link(nc.vector.tensor_tensor(first[:, s, :], rank[:, s, :], over_experts(pick1[:, s]), ALU.is_equal))
                link(nc.vector.scalar_tensor_tensor(rest[:, s, :], first[:, s, :], MASKED, logit[:, s, :],
                                                    ALU.mult, ALU.add))
                link(nc.vector.tensor_reduce(top2[:, s], rest[:, s, :], AX.X, ALU.max))
                nc.vector.tensor_tensor(gap[:, s], top2[:, s], top1[:, s], ALU.subtract).then_inc(gap_set, 1)
                link(nc.vector.tensor_tensor(tied2[:, s, :], rest[:, s, :], over_experts(top2[:, s]), ALU.is_equal))
                link(nc.vector.tensor_tensor(ranked2[:, s, :], tied2[:, s, :], rank[:, s, :], ALU.mult))
                link(nc.vector.tensor_reduce(pick2[:, s], ranked2[:, s, :], AX.X, ALU.max))
                link(nc.vector.tensor_tensor(second[:, s, :], rank[:, s, :], over_experts(pick2[:, s]), ALU.is_equal))
                dve.wait_ge(exp1, g + 1)
                link(nc.vector.tensor_scalar(esum[:, s], egap[:, s], 1.0, 1.0 / SCALING, ALU.add, ALU.mult))
                link(nc.vector.reciprocal(w1[:, s], esum[:, s]))
                link(nc.vector.tensor_tensor(w2[:, s], w1[:, s], egap[:, s], ALU.mult))
                link(nc.vector.tensor_tensor(gate1[:, s, :], first[:, s, :], over_experts(w1[:, s]), ALU.mult))
                link(nc.vector.tensor_tensor(gate2[:, s, :], second[:, s, :], over_experts(w2[:, s]), ALU.mult))
                link(nc.vector.tensor_tensor(g1[:, s, :], gate1[:, s, :], gate2[:, s, :], ALU.add))
                nc.vector.tensor_tensor(hg[:, s, :].rearrange("p t (e r) -> p t e r", e=E),
                                        xn[:, s, 0:ER].rearrange("p t (e r) -> p t e r", e=E),
                                        over_rank(g1[:, s, :]), ALU.mult).then_inc(hg_set, 1)

            def hgT_low(g):
                dve.wait_ge(hg_hi, g + 1)
                minus(hgT_lo[:, group_tok(g)], bank[TR_BANK[g]][:, :], hgT_hi[:, group_tok(g)]).then_inc(hg_lo, 1)

            def hwT_low(g):
                dve.wait_ge(hw_hi, g + 1)
                minus(hwT_lo[:, group_tok(g)], bank[TR_BANK[g]][:, :], hwT_hi[:, group_tok(g)]).then_inc(hw_lo, 1)

            def y2_sum(g):
                for j in range(g * GROUP // PAIR, (g + 1) * GROUP // PAIR):
                    pair = slice(PAIR * j, PAIR * (j + 1))
                    dve.wait_ge(y2_mm, j + 1)
                    nc.vector.tensor_tensor(y2[:, pair, :],
                                            bank[Y2_BANK[j % 2]][:, 0:PAIR * N2].rearrange("p (i c) -> p i c", i=PAIR),
                                            xn[:, pair, N1:NX], ALU.add).then_inc(y2_set, 1)

            def layer2_shift(g):
                s = slice(g * GROUP, (g + 1) * GROUP)
                if g == 0:
                    dve.wait_ge(ld_bthr, 16)
                dve.wait_ge(y2_set, (g + 1) * GROUP // PAIR)
                link(nc.vector.tensor_reduce(top[:, s], y2[:, s, ER:ER + E], AX.X, ALU.max))
                nc.vector.tensor_scalar(shifted[:, s, E], y2[:, s, ER + E], -1.0, bthr_sb[:, 0:1],
                                        ALU.mult, ALU.subtract).then_inc(shift_set, 1)
                nc.vector.tensor_tensor(shifted[:, s, 0:E], y2[:, s, ER:ER + E], over_experts(top[:, s]),
                                        ALU.subtract).then_inc(shift_set, 1)

            def layer2_gates(g):
                s = slice(g * GROUP, (g + 1) * GROUP)
                dve.wait_ge(exp2, g + 1)
                nc.vector.tensor_scalar(den[:, s, 1], ex[:, s, E], 1.0, None, ALU.add).then_inc(step_done, 1)
                steps[0] += 1
                link(nc.vector.tensor_reduce(den[:, s, 0], ex[:, s, 0:E], AX.X, ALU.add))
                link(nc.vector.reciprocal(rden[:, s, :], den[:, s, :]))
                link(nc.vector.tensor_tensor(prob[:, s, :], ex[:, s, 0:E], over_experts(rden[:, s, 0]), ALU.mult))
                link(nc.vector.scalar_tensor_tensor(adapted[:, s, :], over_experts(rden[:, s, 1]), -MAX_THRESHOLD,
                                                    prob[:, s, :], ALU.mult, ALU.add))
                link(nc.vector.tensor_scalar(weight[:, s, :], adapted[:, s, :], 0.0, None, ALU.max))
                link(nc.vector.tensor_reduce(wsum[:, s], weight[:, s, :], AX.X, ALU.add))
                link(nc.vector.scalar_tensor_tensor(wdiv[:, s], wsum[:, s], 0.0, wsum[:, s], ALU.is_equal, ALU.add))
                link(nc.vector.reciprocal(rw[:, s], wdiv[:, s]))
                link(nc.vector.scalar_tensor_tensor(g2[:, s, :], weight[:, s, :], SCALING, over_experts(rw[:, s]),
                                                    ALU.mult, ALU.mult))
                nc.vector.tensor_tensor(hw[:, s, :].rearrange("p t (e r) -> p t e r", e=E),
                                        y2[:, s, 0:ER].rearrange("p t (e r) -> p t e r", e=E),
                                        over_rank(g2[:, s, :]), ALU.mult).then_inc(hw_set, 1)

            def out_sum(t):
                dve.wait_ge(out_mm, t + 1)
                nc.vector.tensor_tensor(out_sb[:, t, :], bank[OUT_BANK[t % RING]][:, :], b_sb[:, :],
                                        ALU.add).then_inc(out_set, 1)

            layer1_gates(0)
            dve.wait_ge(g_hi, 1)
            minus(G_lo[:, :], bank[G_BANK][:, :], G_hi[:, :]).then_inc(g_lo, 1)
            layer1_gates(1)
            hgT_low(0)
            y2_sum(0)
            layer2_shift(0)
            layer2_gates(0)
            hgT_low(1)
            y2_sum(1)
            layer2_shift(1)
            hwT_low(0)
            layer2_gates(1)
            dve.wait_ge(ld_b, 16)
            out_sum(0)
            hwT_low(1)
            for t in range(1, T):
                out_sum(t)


_OUT = "out_0_dram"


def _blocks(m):
    return m.reshape(-1, P, m.shape[1]).transpose(1, 0, 2)


def kernel(**inputs):
    import numpy as _np
    import concourse.bacc as _bacc
    from concourse import mybir as _mybir
    from concourse.bass_utils import run_bass_kernel_spmd as _run

    i = {name: _np.asarray(a) for name, a in inputs.items()}
    batch, seq, d = i["x"].shape
    tokens = batch * seq
    chunk = 2 * P
    e, r, _ = i["L0_cond_A"].shape
    o = i["L0_cond_W"].shape[0]
    x_t = i["x"].reshape(tokens, d).T.reshape(d // P, P, tokens // chunk, chunk).transpose(2, 1, 0, 3)
    narrow1 = _np.concatenate([i["L0_cond_A"].reshape(e * r, d), i["L0_cond_Wr"]])
    narrow2 = _np.concatenate([i["L0_ffn_A"].reshape(e * r, o), i["L0_ffn_W_gate"], i["L0_ffn_W_thr"]])
    laid_out = {
        "xT": x_t,
        "itok": i["itok_B_0_7"].reshape(1, batch),
        "W": _blocks(i["L0_cond_W"]),
        "WbT": _blocks(i["L0_ffn_W_base"].T),
        "narrow1T": _blocks(narrow1.T),
        "narrow2T": _blocks(narrow2.T),
        "B1": _blocks(i["L0_cond_B"].transpose(1, 0, 2).reshape(o, e * r)),
        "B2T": i["L0_ffn_B"].transpose(0, 2, 1).reshape(e * r, -1),
        "b_base": i["L0_ffn_b_base"].reshape(1, -1),
        "b_thr": i["L0_ffn_b_thr"].reshape(1, 1),
    }

    nc = _bacc.Bacc("TRN2", target_bir_lowering=False, num_devices=1)
    arrays, args = {}, []
    for name, a in laid_out.items():
        a = _np.ascontiguousarray(a)
        arrays[f"in_{name}_dram"] = a
        args.append(nc.dram_tensor(f"in_{name}_dram", a.shape, _mybir.dt.from_np(a.dtype), kind="ExternalInput").ap())
    n_out = i["L0_ffn_W_base"].shape[0]
    args.append(nc.dram_tensor(_OUT, (tokens, n_out), F32, kind="ExternalOutput").ap())
    adaln_ffn_kernel(nc, *args)
    result = _run(nc, [arrays], core_ids=[0])
    return result.results[0][_OUT].reshape(batch, seq, n_out)
```

```python
from contextlib import ExitStack

import concourse.bass as bass
from concourse import mybir

ALU = mybir.AluOpType
ACT = mybir.ActivationFunctionType
AX = mybir.AxisListType
F32 = mybir.dt.float32
F32R = mybir.dt.float32r
BF16 = mybir.dt.bfloat16
I32 = mybir.dt.int32

P = 128
LANG_BIAS = 5.0
SCALING = 2.0
MAX_THRESHOLD = 0.125
MASKED = -3.0e38
EXP_FINITE = 87.0
WARM_UP = 32


def adaln_ffn_kernel(nc, xT, itok, W, M1T, M2T, B1, B2T, b_base, b_thr, out):
    CHUNKS, _, K, CT = xT.shape
    _, Q, D = W.shape
    O = out.shape[1]
    ER = B1.shape[2]
    N1 = M1T.shape[2]
    E = N1 - ER
    R = ER // E
    N2 = M2T.shape[2] - O
    T = CHUNKS * CT // P
    TC = CT // P
    GROUP = 4
    PAIR = 2
    NX = N1 + N2
    NF = NX + O
    CUT = (N2 + O) // 4 * 2
    PART = [(0, CUT), (CUT, N2 + O)]
    assert ER == P and out.shape[0] == T * P

    out_tiles = out.rearrange("(t p) o -> t p o", p=P)

    ctx = ExitStack()
    with ctx:
        def sb(name, shape, dt=F32):
            return ctx.enter_context(nc.sbuf_tensor(name, shape, dt))

        def sem(name):
            return ctx.enter_context(nc.semaphore(name))

        xT_sb = sb("xT_sb", [P, K, T * P])
        W_sb = sb("W_sb", [P, Q, D])
        M1T_sb = sb("M1T_sb", [P, K, N1])
        M2T_sb = sb("M2T_sb", [P, Q, N2 + O])
        B1_sb = sb("B1_sb", [P, Q, ER])
        B2T_sb = sb("B2T_sb", [P, O])
        b_sb = sb("b_sb", [P, O])
        bthr_sb = sb("bthr_sb", [P, 1])
        itok_sb = sb("itok_sb", [P, T], I32)

        zeros = sb("zeros", [P, P], BF16)
        ident = sb("ident", [P, P])
        ident_bf = sb("ident_bf", [P, P], BF16)
        xT_hi = sb("xT_hi", [P, K, T * P], F32R)
        xT_lo = sb("xT_lo", [P, K, T * P], F32R)
        W_hi = sb("W_hi", [P, Q, D], F32R)
        W_lo = sb("W_lo", [P, Q, D], F32R)
        M2T_hi = sb("M2T_hi", [P, Q, N2 + O], F32R)
        M2T_lo = sb("M2T_lo", [P, Q, N2 + O], F32R)
        F_hi = sb("F_hi", [P, K, NF], F32R)
        F_lo = sb("F_lo", [P, K, NF], F32R)
        B1_hi = sb("B1_hi", [P, Q, ER], F32R)
        B1_lo = sb("B1_lo", [P, Q, ER], F32R)
        G_narrow = sb("G_narrow", [P, N2])
        G_hi = sb("G_hi", [P, O], F32R)
        G_lo = sb("G_lo", [P, O], F32R)
        B2T_hi = sb("B2T_hi", [P, O], F32R)
        B2T_lo = sb("B2T_lo", [P, O], F32R)
        hgT = sb("hgT", [P, T * P])
        hgT_hi = sb("hgT_hi", [P, T * P], F32R)
        hgT_lo = sb("hgT_lo", [P, T * P], F32R)
        hwT_hi = sb("hwT_hi", [P, T * P], F32R)
        hwT_lo = sb("hwT_lo", [P, T * P], F32R)

        xn = sb("xn", [P, T, NX])
        y2 = sb("y2", [P, T, N2])
        hg = sb("hg", [P, T, ER])
        hw = sb("hw", [P, T, ER])
        expert = sb("expert", [P, T, E], I32)
        rank = sb("rank", [P, T, E])
        spoken = sb("spoken", [P, T, E])
        logit = sb("logit", [P, T, E])
        tied1, first, rest, tied2, second = (sb(n, [P, T, E]) for n in ("tied1", "first", "rest", "tied2", "second"))
        ranked1, ranked2, gate1, gate2, g1 = (sb(n, [P, T, E]) for n in ("ranked1", "ranked2", "gate1", "gate2", "g1"))
        top1, top2, pick1, pick2 = (sb(n, [P, T]) for n in ("top1", "top2", "pick1", "pick2"))
        gap, egap, esum, w1, w2 = (sb(n, [P, T]) for n in ("gap", "egap", "esum", "w1", "w2"))
        top, negated = sb("top", [P, T]), sb("negated", [P, T])
        shifted = sb("shifted", [P, T, E + 1])
        ex = sb("ex", [P, T, E + 1])
        den = sb("den", [P, T, 2])
        rden = sb("rden", [P, T, 2])
        prob, adapted, weight, g2 = (sb(n, [P, T, E]) for n in ("prob", "adapted", "weight", "g2"))
        wsum, wdiv, rw = (sb(n, [P, T]) for n in ("wsum", "wdiv", "rw"))
        out_sb = xT_sb[:, :, :].rearrange("p k n -> p (k n)").rearrange("p (t o) -> p t o", o=O)

        bank = [ctx.enter_context(nc.psum_tensor(f"bank{i}", [P, 512], F32)) for i in range(8)]
        F_BANK = [[0, 1, 2, 3], [4, 5, 6, 7]]
        XN_BANK = [0, 1]
        G_BANK = [2, 3]
        TR_BANK = [2, 3]
        Y2_BANK = [0, 1]
        OUT_BANK = [4, 5, 6, 7, 0, 1]
        RING = len(OUT_BANK)
        HALF = O // 2
        HALF_BANK = [OUT_BANK[(T - 1) % RING], TR_BANK[0]]

        ld_m1, ld_b1, ld_b2, ld_b, ld_bthr, ld_itok = map(sem, (
            "ld_m1", "ld_b1", "ld_b2", "ld_b", "ld_bthr", "ld_itok"))
        ld_w = [sem(f"ld_w{q}") for q in range(Q)]
        ld_m2 = [[sem(f"ld_m2{q}_{i}") for i in range(2)] for q in range(Q)]
        ld_x = [sem(f"ld_x{c}") for c in range(CHUNKS)]
        stored = sem("stored")
        f_mm, xn_mm, g_mm, y2_mm, out_mm, hg_T, hw_T = map(sem, (
            "f_mm", "xn_mm", "g_mm", "y2_mm", "out_mm", "hg_T", "hw_T"))
        m2_hi, m1_hi, x_hi, f_hi, xn_sc, gn_sc, g_hi, hg_sc, hg_hi, hw_hi, exp1, exp2 = map(sem, (
            "m2_hi", "m1_hi", "x_hi", "f_hi", "xn_sc", "gn_sc", "g_hi", "hg_sc", "hg_hi", "hw_hi", "exp1", "exp2"))
        zeros_set, w_hi, w_lo, m2_lo, m1_lo, x_lo, f_lo, g_lo, hg_lo, hw_lo = map(sem, (
            "zeros_set", "w_hi", "w_lo", "m2_lo", "m1_lo", "x_lo", "f_lo", "g_lo", "hg_lo", "hw_lo"))
        gap_set, hg_set, y2_set, shift_set, hw_set, out_set, step_done = map(sem, (
            "gap_set", "hg_set", "y2_set", "shift_set", "hw_set", "out_set", "step_done"))
        ident_zero, ident_set, ident_bf_set, iota_set, rank_set, b1_hi, b1_lo, b2_hi, b2_lo = map(sem, (
            "ident_zero", "ident_set", "ident_bf_set", "iota_set", "rank_set", "b1_hi", "b1_lo", "b2_hi", "b2_lo"))

        def tok(t):
            return slice(t * P, (t + 1) * P)

        def group_tok(g):
            return slice(g * GROUP * P, (g + 1) * GROUP * P)

        def chunk_tok(c):
            return slice(c * CT, (c + 1) * CT)

        block = ctx.enter_context(nc.Block())

        @block.sync
        def _(sp):
            for q in range(Q):
                for i, (a, b) in enumerate(PART):
                    sp.dma_start(M2T_sb[:, q, a:b], M2T[:, q, a:b]).then_inc(ld_m2[q][i], 16)
                    if i == 0:
                        sp.dma_start(W_sb[:, q, :], W[:, q, :]).then_inc(ld_w[q], 16)
            sp.dma_start(xT_sb[:, :, chunk_tok(0)], xT[0]).then_inc(ld_x[0], 16)
            sp.dma_start(M1T_sb[:, :, :], M1T).then_inc(ld_m1, 16)
            for c in range(1, CHUNKS):
                sp.dma_start(xT_sb[:, :, chunk_tok(c)], xT[c]).then_inc(ld_x[c], 16)
            sp.dma_start(B1_sb[:, :, :], B1).then_inc(ld_b1, 16)
            sp.dma_start(itok_sb[:, :], itok.broadcast_to([P, T])).then_inc(ld_itok, 16)
            sp.dma_start(bthr_sb[:, :], b_thr.broadcast_to([P, 1])).then_inc(ld_bthr, 16)
            sp.dma_start(B2T_sb[:, :], B2T).then_inc(ld_b2, 16)
            sp.dma_start(b_sb[:, :], b_base.broadcast_to([P, O])).then_inc(ld_b, 16)
            with sp.Fori(0, T - 2) as t:
                sp.wait_ge(out_set, t + 1)
                sp.dma_start(out_tiles[bass.ds(t, 1)], out_sb[:, bass.ds(t, 1), :]).then_inc(stored, 16)
            sp.wait_ge(out_set, T - 1)
            sp.dma_start(out_tiles[T - 2], out_sb[:, T - 2, :]).then_inc(stored, 16)
            for h in range(2):
                half = slice(h * HALF, (h + 1) * HALF)
                sp.wait_ge(out_set, T + h)
                sp.dma_start(out_tiles[T - 1, :, half], out_sb[:, T - 1, half]).then_inc(stored, 16)
            sp.wait_ge(stored, 16 * (T + 1))

        @block.gpsimd
        def _(pool):
            nc.gpsimd.memset(ident[:, :], 0.0).then_inc(ident_zero, 1)
            pool.wait_ge(ident_zero, 1)
            nc.gpsimd.affine_select(out=ident[:, :], in_=ident[:, :], compare_op=ALU.not_equal, fill=1.0,
                                    base=0, pattern=[[-1, P]], channel_multiplier=1).then_inc(ident_set, 1)
            pool.wait_ge(ident_set, 1)
            nc.gpsimd.tensor_copy(ident_bf[:, :], ident[:, :]).then_inc(ident_bf_set, 1)
            nc.gpsimd.iota(expert[:, :, :], pattern=[[0, T], [1, E]], base=0, channel_multiplier=0).then_inc(iota_set, 1)
            pool.wait_ge(iota_set, 1)
            nc.gpsimd.tensor_scalar(rank[:, :, :], expert[:, :, :], -1.0, float(E), ALU.mult, ALU.add).then_inc(rank_set, 1)
            for ld, whole, hi, lo, hi_set, lo_set in (
                    (ld_b1, B1_sb[:, :, :], B1_hi[:, :, :], B1_lo[:, :, :], b1_hi, b1_lo),
                    (ld_b2, B2T_sb[:, :], B2T_hi[:, :], B2T_lo[:, :], b2_hi, b2_lo)):
                pool.wait_ge(ld, 16)
                nc.gpsimd.tensor_copy(hi, whole).then_inc(hi_set, 1)
                pool.wait_ge(hi_set, 1)
                nc.gpsimd.tensor_tensor(lo, whole, hi.bitcast(F32), ALU.subtract).then_inc(lo_set, 1)

        @block.scalar
        def _(act):
            nc.scalar.preload_act_table(ACT.Exp)

            def copy(dst, src):
                return nc.scalar.copy(dst, src)

            for q in range(Q):
                for i, (a, b) in enumerate(PART):
                    act.wait_ge(ld_m2[q][i], 16)
                    copy(M2T_hi[:, q, a:b], M2T_sb[:, q, a:b]).then_inc(m2_hi, 1)
            for c in range(CHUNKS):
                act.wait_ge(ld_x[c], 16)
                copy(xT_hi[:, :, chunk_tok(c)], xT_sb[:, :, chunk_tok(c)]).then_inc(x_hi, 1)
                if c == 0:
                    act.wait_ge(ld_m1, 16)
                    copy(F_hi[:, :, 0:N1], M1T_sb[:, :, :]).then_inc(m1_hi, 1)

            def f_part(i, k):
                a, b = PART[i]
                act.wait_ge(f_mm, i * K + k + 1)
                copy(F_hi[:, k, N1 + a:N1 + b], bank[F_BANK[i][k]][:, 0:b - a]).then_inc(f_hi, 1)

            for k in range(K):
                f_part(0, k)

            def xn_copy(t):
                act.wait_ge(xn_mm, t + 1)
                copy(xn[:, t, :], bank[XN_BANK[t % 2]][:, 0:NX]).then_inc(xn_sc, 1)

            def hgT_copy(g):
                act.wait_ge(hg_T, g + 1)
                copy(hgT[:, group_tok(g)], bank[TR_BANK[g]][:, :]).then_inc(hg_sc, 1)
                copy(hgT_hi[:, group_tok(g)], bank[TR_BANK[g]][:, :]).then_inc(hg_hi, 1)

            def exp_gap(g):
                act.wait_ge(gap_set, g + 1)
                nc.scalar.activation(egap[:, g * GROUP:(g + 1) * GROUP], gap[:, g * GROUP:(g + 1) * GROUP],
                                     ACT.Exp).then_inc(exp1, 1)

            def exp_shifted(g):
                act.wait_ge(shift_set, 2 * (g + 1))
                nc.scalar.activation(ex[:, g * GROUP:(g + 1) * GROUP, :], shifted[:, g * GROUP:(g + 1) * GROUP, :],
                                     ACT.Exp).then_inc(exp2, 1)

            def hwT_copy(g):
                act.wait_ge(hw_T, g + 1)
                copy(hwT_hi[:, group_tok(g)], bank[TR_BANK[g]][:, :]).then_inc(hw_hi, 1)

            for t in range(GROUP):
                f_part(1, t)
                xn_copy(t)
            exp_gap(0)
            act.wait_ge(g_mm, 1)
            copy(G_narrow[:, :], bank[G_BANK[0]][:, 0:N2]).then_inc(gn_sc, 1)
            copy(G_hi[:, 0:CUT - N2], bank[G_BANK[0]][:, N2:CUT]).then_inc(g_hi, 1)
            act.wait_ge(g_mm, 2)
            copy(G_hi[:, CUT - N2:O], bank[G_BANK[1]][:, 0:N2 + O - CUT]).then_inc(g_hi, 1)
            for t in range(GROUP, T):
                xn_copy(t)
            hgT_copy(0)
            exp_gap(1)
            hgT_copy(1)
            exp_shifted(0)
            hwT_copy(0)
            exp_shifted(1)
            hwT_copy(1)

        @block.tensor
        def _(pe):
            def product(dst, terms, first=True, last=True):
                for n, (lhsT, rhs) in enumerate(terms):
                    mm = nc.tensor.matmul(dst, lhsT, rhs, start=first and n == 0, stop=last and n == len(terms) - 1)
                return mm

            def three(a_hi, a_lo, b_hi, b_lo):
                return [(a_hi, b_hi), (a_hi, b_lo), (a_lo, b_hi)]

            pe.wait_ge(zeros_set, 1)
            for _ in range(WARM_UP):
                nc.tensor.matmul(bank[0][:, 0:P], zeros[:, :], zeros[:, :], start=True, stop=True)

            def f_pass(q, k, i, W_part, M2T_part, first=False, last=False):
                a, b = PART[i]
                return nc.tensor.matmul(bank[F_BANK[i][k]][:, 0:b - a], W_part[:, q, k * P:(k + 1) * P],
                                        M2T_part[:, q, a:b], start=first, stop=last)

            def f_identity(k, i):
                (a, b), at = PART[i], N2 + k * P
                a0, b0 = max(at, a), min(at + P, b)
                return nc.tensor.matmul(bank[F_BANK[i][k]][:, a0 - a:b0 - a], ident_bf[:, :],
                                        ident_bf[:, a0 - at:b0 - at], start=False, stop=False)

            def crosses(k, i):
                return max(N2 + k * P, PART[i][0]) < min(N2 + (k + 1) * P, PART[i][1])

            for q in range(Q):
                pe.wait_ge(w_hi, q + 1)
                for i in range(2):
                    pe.wait_ge(m2_hi, 2 * q + i + 1)
                    for k in range(K):
                        f_pass(q, k, i, W_hi, M2T_hi, first=q == 0)
                if q == Q - 1:
                    pe.wait_ge(ident_bf_set, 1)
                    for i in range(2):
                        for k in range(K):
                            if crosses(k, i):
                                f_identity(k, i)
                pe.wait_ge(w_lo, q + 1)
                for i in range(2):
                    pe.wait_ge(m2_lo, 2 * q + i + 1)
                    for k in range(K):
                        f_pass(q, k, i, W_hi, M2T_lo)
                        mm = f_pass(q, k, i, W_lo, M2T_hi, last=q == Q - 1)
                        if q == Q - 1:
                            mm.then_inc(f_mm, 1)

            def x_narrow(t):
                pe.wait_ge(x_lo, t // TC + 1)
                if t == 0:
                    pe.wait_ge(m1_lo, 1)
                if t >= 2:
                    pe.wait_ge(xn_sc, t - 1)
                for k in range(K):
                    if t == 0:
                        pe.wait_ge(f_lo, k + 1)
                    last = product(bank[XN_BANK[t % 2]][:, 0:NX],
                                   three(xT_hi[:, k, tok(t)], xT_lo[:, k, tok(t)], F_hi[:, k, 0:NX], F_lo[:, k, 0:NX]),
                                   first=k == 0, last=k == K - 1)
                last.then_inc(xn_mm, 1)

            def transpose_group(h, g):
                for i in range(GROUP):
                    last = nc.tensor.transpose(bank[TR_BANK[g]][:, i * P:(i + 1) * P], h[:, g * GROUP + i, :], ident[:, :])
                return last

            def transpose_hg(g):
                pe.wait_ge(hg_set, g + 1)
                if g == 0:
                    pe.wait_ge(ident_set, 1)
                pe.wait_ge(g_lo, g + 1)
                transpose_group(hg, g).then_inc(hg_T, 1)

            def transpose_hw(g):
                pe.wait_ge(hw_set, g + 1)
                pe.wait_ge(hg_lo, g + 1)
                transpose_group(hw, g).then_inc(hw_T, 1)

            def y2_group(g):
                pe.wait_ge(gn_sc, 1)
                pe.wait_ge(hg_sc, g + 1)
                for j in range(g * GROUP // PAIR, (g + 1) * GROUP // PAIR):
                    if j < 2:
                        pe.wait_ge(xn_sc, T - 1 + j)
                    else:
                        pe.wait_ge(y2_set, j - 1)
                    for i in range(PAIR):
                        last = nc.tensor.matmul(bank[Y2_BANK[j % 2]][:, i * N2:(i + 1) * N2],
                                                hgT[:, tok(PAIR * j + i)], G_narrow[:, :], start=True, stop=True)
                    last.then_inc(y2_mm, 1)

            def out_x(t):
                if t < K:
                    pe.wait_ge(f_lo, 2 * K)
                elif t < RING:
                    pe.wait_ge(y2_set, T // PAIR - RING + 1 + t)
                else:
                    pe.wait_ge(out_set, t - RING + 1)
                if t < T - 1:
                    parts = [(bank[OUT_BANK[t % RING]][:, :], slice(NX, NF))]
                else:
                    pe.wait_ge(hw_lo, 1)
                    parts = [(bank[HALF_BANK[h]][:, 0:HALF], slice(NX + h * HALF, NX + (h + 1) * HALF)) for h in range(2)]
                for dst, cols in parts:
                    terms = []
                    for k in range(K):
                        terms += three(xT_hi[:, k, tok(t)], xT_lo[:, k, tok(t)], F_hi[:, k, cols], F_lo[:, k, cols])
                    product(dst, terms, last=False)

            def lora(dst, t, cols):
                product(dst,
                        three(hgT_hi[:, tok(t)], hgT_lo[:, tok(t)], G_hi[:, cols], G_lo[:, cols])
                        + three(hwT_hi[:, tok(t)], hwT_lo[:, tok(t)], B2T_hi[:, cols], B2T_lo[:, cols]),
                        first=False).then_inc(out_mm, 1)

            def out_lora(t):
                if t == 0:
                    pe.wait_ge(b2_lo, 1)
                pe.wait_ge(hw_lo, t // GROUP + 1)
                if t < T - 1:
                    lora(bank[OUT_BANK[t % RING]][:, :], t, slice(0, O))
                else:
                    for h in range(2):
                        lora(bank[HALF_BANK[h]][:, 0:HALF], t, slice(h * HALF, (h + 1) * HALF))

            for t in range(GROUP):
                x_narrow(t)
            pe.wait_ge(b1_lo, 1)
            for (a, b), n in zip(PART, G_BANK):
                terms = []
                for q in range(Q):
                    terms += three(B1_hi[:, q, :], B1_lo[:, q, :], M2T_hi[:, q, a:b], M2T_lo[:, q, a:b])
                product(bank[n][:, 0:b - a], terms).then_inc(g_mm, 1)
            for t in range(GROUP, T):
                x_narrow(t)
            transpose_hg(0)
            out_x(0)
            y2_group(0)
            out_x(1)
            transpose_hg(1)
            out_x(2)
            y2_group(1)
            out_x(3)
            transpose_hw(0)
            out_x(4)
            out_lora(0)
            out_lora(1)
            transpose_hw(1)
            for t in range(5, T):
                out_x(t)
                out_lora(t - 3)
            for t in range(T - 3, T):
                out_lora(t)

        @block.vector
        def _(dve):
            steps = [0]

            def link(ins):
                steps[0] += 1
                ins.then_inc(step_done, 1)
                dve.wait_ge(step_done, steps[0])

            def minus(lo, whole, hi):
                return nc.vector.tensor_tensor(lo, whole, hi.bitcast(F32), ALU.subtract)

            def over_experts(v):
                return v.unsqueeze(2).broadcast_to([P, v.shape[1], E])

            def over_rank(v):
                return v.unsqueeze(3).broadcast_to([P, v.shape[1], E, R])

            nc.vector.memset(zeros[:, :], 0.0).then_inc(zeros_set, 1)
            for q in range(Q):
                dve.wait_ge(ld_w[q], 16)
                nc.vector.tensor_copy(W_hi[:, q, :], W_sb[:, q, :]).then_inc(w_hi, 1)
                for i, (a, b) in enumerate(PART):
                    dve.wait_ge(m2_hi, 2 * q + i + 1)
                    minus(M2T_lo[:, q, a:b], M2T_sb[:, q, a:b], M2T_hi[:, q, a:b]).then_inc(m2_lo, 1)
                    if i == 0:
                        dve.wait_ge(w_hi, q + 1)
                        minus(W_lo[:, q, :], W_sb[:, q, :], W_hi[:, q, :]).then_inc(w_lo, 1)
            def x_low(c):
                dve.wait_ge(x_hi, c + 1)
                minus(xT_lo[:, :, chunk_tok(c)], xT_sb[:, :, chunk_tok(c)], xT_hi[:, :, chunk_tok(c)]).then_inc(x_lo, 1)

            def f_low(i):
                a, b = PART[i]
                for k in range(K):
                    dve.wait_ge(f_hi, i * K + k + 1)
                    minus(F_lo[:, k, N1 + a:N1 + b], bank[F_BANK[i][k]][:, 0:b - a],
                          F_hi[:, k, N1 + a:N1 + b]).then_inc(f_lo, 1)

            x_low(0)
            dve.wait_ge(m1_hi, 1)
            minus(F_lo[:, :, 0:N1], M1T_sb[:, :, :], F_hi[:, :, 0:N1]).then_inc(m1_lo, 1)
            x_low(1)
            f_low(0)
            for c in range(2, CHUNKS):
                x_low(c)
            f_low(1)
            dve.wait_ge(ld_itok, 16)
            dve.wait_ge(iota_set, 1)
            link(nc.vector.tensor_tensor(spoken[:, :, :], over_experts(itok_sb[:, :]), expert[:, :, :], ALU.is_equal))

            def layer1_gates(g):
                s = slice(g * GROUP, (g + 1) * GROUP)
                dve.wait_ge(xn_sc, (g + 1) * GROUP)
                link(nc.vector.scalar_tensor_tensor(logit[:, s, :], spoken[:, s, :], LANG_BIAS, xn[:, s, ER:N1],
                                                    ALU.mult, ALU.add))
                link(nc.vector.tensor_reduce(top1[:, s], logit[:, s, :], AX.X, ALU.max))
                link(nc.vector.tensor_tensor(tied1[:, s, :], logit[:, s, :], over_experts(top1[:, s]), ALU.is_equal))
                if g == 0:
                    dve.wait_ge(rank_set, 1)
                link(nc.vector.tensor_tensor(ranked1[:, s, :], tied1[:, s, :], rank[:, s, :], ALU.mult))
                link(nc.vector.tensor_reduce(pick1[:, s], ranked1[:, s, :], AX.X, ALU.max))
                link(nc.vector.tensor_tensor(first[:, s, :], rank[:, s, :], over_experts(pick1[:, s]), ALU.is_equal))
                link(nc.vector.scalar_tensor_tensor(rest[:, s, :], first[:, s, :], MASKED, logit[:, s, :],
                                                    ALU.mult, ALU.add))
                link(nc.vector.tensor_reduce(top2[:, s], rest[:, s, :], AX.X, ALU.max))
                nc.vector.tensor_tensor(gap[:, s], top2[:, s], top1[:, s], ALU.subtract).then_inc(gap_set, 1)
                link(nc.vector.tensor_tensor(tied2[:, s, :], rest[:, s, :], over_experts(top2[:, s]), ALU.is_equal))
                link(nc.vector.tensor_tensor(ranked2[:, s, :], tied2[:, s, :], rank[:, s, :], ALU.mult))
                link(nc.vector.tensor_reduce(pick2[:, s], ranked2[:, s, :], AX.X, ALU.max))
                link(nc.vector.tensor_tensor(second[:, s, :], rank[:, s, :], over_experts(pick2[:, s]), ALU.is_equal))
                dve.wait_ge(exp1, g + 1)
                link(nc.vector.tensor_scalar(esum[:, s], egap[:, s], 1.0, 1.0 / SCALING, ALU.add, ALU.mult))
                link(nc.vector.reciprocal(w1[:, s], esum[:, s]))
                link(nc.vector.tensor_tensor(w2[:, s], w1[:, s], egap[:, s], ALU.mult))
                link(nc.vector.tensor_tensor(gate1[:, s, :], first[:, s, :], over_experts(w1[:, s]), ALU.mult))
                link(nc.vector.tensor_tensor(gate2[:, s, :], second[:, s, :], over_experts(w2[:, s]), ALU.mult))
                link(nc.vector.tensor_tensor(g1[:, s, :], gate1[:, s, :], gate2[:, s, :], ALU.add))
                nc.vector.tensor_tensor(hg[:, s, :].rearrange("p t (e r) -> p t e r", e=E),
                                        xn[:, s, 0:ER].rearrange("p t (e r) -> p t e r", e=E),
                                        over_rank(g1[:, s, :]), ALU.mult).then_inc(hg_set, 1)

            def hgT_low(g):
                dve.wait_ge(hg_hi, g + 1)
                minus(hgT_lo[:, group_tok(g)], bank[TR_BANK[g]][:, :], hgT_hi[:, group_tok(g)]).then_inc(hg_lo, 1)

            def hwT_low(g):
                dve.wait_ge(hw_hi, g + 1)
                minus(hwT_lo[:, group_tok(g)], bank[TR_BANK[g]][:, :], hwT_hi[:, group_tok(g)]).then_inc(hw_lo, 1)

            def y2_sum(g):
                for j in range(g * GROUP // PAIR, (g + 1) * GROUP // PAIR):
                    pair = slice(PAIR * j, PAIR * (j + 1))
                    dve.wait_ge(y2_mm, j + 1)
                    nc.vector.tensor_tensor(y2[:, pair, :],
                                            bank[Y2_BANK[j % 2]][:, 0:PAIR * N2].rearrange("p (i c) -> p i c", i=PAIR),
                                            xn[:, pair, N1:NX], ALU.add).then_inc(y2_set, 1)

            def layer2_shift(g):
                s = slice(g * GROUP, (g + 1) * GROUP)
                if g == 0:
                    dve.wait_ge(ld_bthr, 16)
                dve.wait_ge(y2_set, (g + 1) * GROUP // PAIR)
                link(nc.vector.tensor_reduce(top[:, s], y2[:, s, ER:ER + E], AX.X, ALU.max))
                link(nc.vector.tensor_scalar(negated[:, s], y2[:, s, ER + E], -1.0, bthr_sb[:, 0:1],
                                             ALU.mult, ALU.subtract))
                nc.vector.tensor_scalar(shifted[:, s, E], negated[:, s], EXP_FINITE, None,
                                        ALU.min).then_inc(shift_set, 1)
                nc.vector.tensor_tensor(shifted[:, s, 0:E], y2[:, s, ER:ER + E], over_experts(top[:, s]),
                                        ALU.subtract).then_inc(shift_set, 1)

            def layer2_gates(g):
                s = slice(g * GROUP, (g + 1) * GROUP)
                dve.wait_ge(exp2, g + 1)
                nc.vector.tensor_scalar(den[:, s, 1], ex[:, s, E], 1.0, None, ALU.add).then_inc(step_done, 1)
                steps[0] += 1
                link(nc.vector.tensor_reduce(den[:, s, 0], ex[:, s, 0:E], AX.X, ALU.add))
                link(nc.vector.reciprocal(rden[:, s, :], den[:, s, :]))
                link(nc.vector.tensor_tensor(prob[:, s, :], ex[:, s, 0:E], over_experts(rden[:, s, 0]), ALU.mult))
                link(nc.vector.scalar_tensor_tensor(adapted[:, s, :], over_experts(rden[:, s, 1]), -MAX_THRESHOLD,
                                                    prob[:, s, :], ALU.mult, ALU.add))
                link(nc.vector.tensor_scalar(weight[:, s, :], adapted[:, s, :], 0.0, None, ALU.max))
                link(nc.vector.tensor_reduce(wsum[:, s], weight[:, s, :], AX.X, ALU.add))
                link(nc.vector.scalar_tensor_tensor(wdiv[:, s], wsum[:, s], 0.0, wsum[:, s], ALU.is_equal, ALU.add))
                link(nc.vector.reciprocal(rw[:, s], wdiv[:, s]))
                link(nc.vector.scalar_tensor_tensor(g2[:, s, :], weight[:, s, :], SCALING, over_experts(rw[:, s]),
                                                    ALU.mult, ALU.mult))
                nc.vector.tensor_tensor(hw[:, s, :].rearrange("p t (e r) -> p t e r", e=E),
                                        y2[:, s, 0:ER].rearrange("p t (e r) -> p t e r", e=E),
                                        over_rank(g2[:, s, :]), ALU.mult).then_inc(hw_set, 1)

            def out_sum(t):
                dve.wait_ge(out_mm, t + 1)
                nc.vector.tensor_tensor(out_sb[:, t, :], bank[OUT_BANK[t % RING]][:, :], b_sb[:, :],
                                        ALU.add).then_inc(out_set, 1)

            layer1_gates(0)
            dve.wait_ge(g_hi, 1)
            minus(G_lo[:, 0:CUT - N2], bank[G_BANK[0]][:, N2:CUT], G_hi[:, 0:CUT - N2]).then_inc(g_lo, 1)
            dve.wait_ge(g_hi, 2)
            minus(G_lo[:, CUT - N2:O], bank[G_BANK[1]][:, 0:N2 + O - CUT], G_hi[:, CUT - N2:O]).then_inc(g_lo, 1)
            layer1_gates(1)
            hgT_low(0)
            y2_sum(0)
            layer2_shift(0)
            layer2_gates(0)
            hgT_low(1)
            y2_sum(1)
            layer2_shift(1)
            hwT_low(0)
            layer2_gates(1)
            dve.wait_ge(ld_b, 16)
            out_sum(0)
            hwT_low(1)
            for t in range(1, T - 1):
                out_sum(t)
            for h in range(2):
                half = slice(h * HALF, (h + 1) * HALF)
                dve.wait_ge(out_mm, T + h)
                nc.vector.tensor_tensor(out_sb[:, T - 1, half], bank[HALF_BANK[h]][:, 0:HALF], b_sb[:, half],
                                        ALU.add).then_inc(out_set, 1)


_OUT = "out_0_dram"


def _blocks(m):
    return m.reshape(-1, P, m.shape[1]).transpose(1, 0, 2)


def kernel(**inputs):
    import numpy as _np
    import concourse.bacc as _bacc
    from concourse import mybir as _mybir
    from concourse.bass_utils import run_bass_kernel_spmd as _run

    i = {name: _np.asarray(a) for name, a in inputs.items()}
    batch, seq, d = i["x"].shape
    tokens = batch * seq
    chunk = 2 * P
    e, r, _ = i["L0_cond_A"].shape
    o = i["L0_cond_W"].shape[0]
    x_t = i["x"].reshape(tokens, d).T.reshape(d // P, P, tokens // chunk, chunk).transpose(2, 1, 0, 3)
    m1 = _np.concatenate([i["L0_cond_A"].reshape(e * r, d), i["L0_cond_Wr"]])
    narrow2 = _np.concatenate([i["L0_ffn_A"].reshape(e * r, o), i["L0_ffn_W_gate"], i["L0_ffn_W_thr"]])
    m2 = _np.concatenate([_np.pad(narrow2, ((0, len(narrow2) % 2), (0, 0))), i["L0_ffn_W_base"]])
    laid_out = {
        "xT": x_t,
        "itok": i["itok_B_0_7"].reshape(1, batch),
        "W": _blocks(i["L0_cond_W"]),
        "M1T": _blocks(m1.T),
        "M2T": _blocks(m2.T),
        "B1": _blocks(i["L0_cond_B"].transpose(1, 0, 2).reshape(o, e * r)),
        "B2T": i["L0_ffn_B"].transpose(0, 2, 1).reshape(e * r, -1),
        "b_base": i["L0_ffn_b_base"].reshape(1, -1),
        "b_thr": i["L0_ffn_b_thr"].reshape(1, 1),
    }

    nc = _bacc.Bacc("TRN2", target_bir_lowering=False, num_devices=1)
    arrays, args = {}, []
    for name, a in laid_out.items():
        a = _np.ascontiguousarray(a)
        arrays[f"in_{name}_dram"] = a
        args.append(nc.dram_tensor(f"in_{name}_dram", a.shape, _mybir.dt.from_np(a.dtype), kind="ExternalInput").ap())
    n_out = i["L0_ffn_W_base"].shape[0]
    args.append(nc.dram_tensor(_OUT, (tokens, n_out), F32, kind="ExternalOutput").ap())
    adaln_ffn_kernel(nc, *args)
    result = _run(nc, [arrays], core_ids=[0])
    return result.results[0][_OUT].reshape(batch, seq, n_out)
```
